# Optimizing a Trainium2 kernel written in Bass

```python
import numpy as np
import jax
import jax.numpy as jnp

def _softmax(x, axis=-1):
    return jax.nn.softmax(x, axis=axis)

def _gelu(x):
    return jax.nn.gelu(x, approximate=True)

def _silu(x):
    return jax.nn.silu(x)

def _sigmoid(x):
    return jax.nn.sigmoid(x)

def _layernorm(x, axis=-1, eps=1e-05):
    m = jnp.mean(x, axis=axis, keepdims=True)
    v = jnp.var(x, axis=axis, keepdims=True)
    return (x - m) / jnp.sqrt(v + eps)

def _scatter_add(tgt, idx, src, axis=0):
    return tgt.at[idx].add(src)

def _segment_sum(src, seg, n):
    return jax.ops.segment_sum(src, seg, n)
kernel_name = 'mk_sandwich_d1_jaxref_r8_15f12c'

def setup_inputs(seed: int=0):
    np.random.seed(seed)
    _w = jnp.asarray

    def _L0_attn_setup():
        import jax, jax.numpy as jnp
        import numpy as np
        D_MODEL = 128
        N_HEADS = 32
        HEAD_DIM = D_MODEL // N_HEADS
        EPS = 1e-05
        key = jax.random.key(seed)
        ks = jax.random.split(key, 6)
        B, S = (2, 256)
        scale = 1.0 / np.sqrt(D_MODEL)
        return {'x': jax.random.normal(ks[0], (B, S, D_MODEL), dtype=jnp.float32), 'Wqkv_w': jax.random.normal(ks[1], (3 * D_MODEL, D_MODEL), dtype=jnp.float32) * scale, 'Wqkv_b': jax.random.normal(ks[2], (3 * D_MODEL,), dtype=jnp.float32) * 0.01, 'gn_w': jnp.ones((D_MODEL,), dtype=jnp.float32), 'gn_b': jnp.zeros((D_MODEL,), dtype=jnp.float32), 'out_w': jax.random.normal(ks[3], (D_MODEL, D_MODEL), dtype=jnp.float32) * scale, 'out_b': jax.random.normal(ks[4], (D_MODEL,), dtype=jnp.float32) * 0.01}
    _L0_attn_in = _L0_attn_setup()

    def _L0_ffn_setup():
        import jax, jax.numpy as jnp
        import numpy as np
        DIM = 128
        DEPTH = 6
        HEADS = 16
        DIM_HEAD = 64
        WINDOW = 32
        INNER = HEADS * DIM_HEAD
        DIM_INNER = int(DIM * 4 * 2 / 3)
        QK_SCALE = 8.0

        def shift_tokens(t):
            a, s = jnp.split(t, 2, -1)
            s = jnp.pad(s, ((0, 0), (1, 0), (0, 0)))[:, :-1]
            return jnp.concatenate([a, s], -1)

        def l2norm(t):
            return t / jnp.maximum(jnp.linalg.norm(t, axis=-1, keepdims=True), 1e-12)

        def rotate_half(x):
            x1, x2 = jnp.split(x, 2, -1)
            return jnp.concatenate([-x2, x1], -1)

        def rotary_tables(n):
            half = jnp.arange(0, DIM_HEAD, 2, dtype=jnp.float32)
            inv_freq = 1.0 / 10000.0 ** (half / DIM_HEAD)
            t = jnp.arange(n, dtype=jnp.float32)
            freqs = t[:, None] * inv_freq[None, :]
            freqs = jnp.concatenate([freqs, freqs], -1)
            base_scale = (half + 0.4 * DIM_HEAD) / (1.4 * DIM_HEAD)
            power = (t - n // 2) / (WINDOW // 2)
            scale = base_scale[None, :] ** power[:, None]
            scale = jnp.concatenate([scale, scale], -1)
            return (freqs, scale)

        def local_attention(q, k, v):
            b, h, n, d = q.shape
            w = WINDOW
            nw = n // w
            bq = q.reshape(b, h, nw, w, d)
            bk = k.reshape(b, h, nw, w, d)
            bv = v.reshape(b, h, nw, w, d)

            def look(t):
                p = jnp.pad(t, ((0, 0), (0, 0), (1, 0), (0, 0), (0, 0)))
                return jnp.concatenate([p[:, :, :nw], p[:, :, 1:]], axis=3)
            bk2, bv2 = (look(bk), look(bv))
            seq = jnp.arange(n).reshape(nw, w)
            seq_p = jnp.pad(seq, ((1, 0), (0, 0)), constant_values=-1)
            jt = jnp.concatenate([seq_p[:nw], seq_p[1:]], axis=1)
            it = seq[:, :, None]
            jb = jt[:, None, :]
            mask = (it < jb) | (it > jb + w) | (jb == -1)
            sim = jnp.einsum('bhwie,bhwje->bhwij', bq, bk2) * QK_SCALE
            sim = jnp.where(mask, -jnp.finfo(sim.dtype).max, sim)
            attn = jax.nn.softmax(sim, -1)
            out = jnp.einsum('bhwij,bhwje->bhwie', attn, bv2)
            return out.reshape(b, h, n, d)

        def attn_layer(x, Wqkv, qs, ksc, Wo):
            b, n, _ = x.shape
            qkv = x @ Wqkv
            q, k, v = jnp.split(qkv, 3, -1)
            sh = lambda t: t.reshape(b, n, HEADS, DIM_HEAD).transpose(0, 2, 1, 3)
            q, k, v = (sh(q), sh(k), sh(v))
            q = l2norm(q) * qs
            k = l2norm(k) * ksc
            freqs, scale = rotary_tables(n)
            cos, sin = (jnp.cos(freqs), jnp.sin(freqs))
            q = q * cos * scale + rotate_half(q) * sin * scale
            inv = 1.0 / scale
            k = k * cos * inv + rotate_half(k) * sin * inv
            out = local_attention(q, k, v)
            out = out.transpose(0, 2, 1, 3).reshape(b, n, INNER)
            return out @ Wo

        def ffn_layer(x, g, bln, W1, b1, W2, b2):
            mu = x.mean(-1, keepdims=True)
            var = ((x - mu) ** 2).mean(-1, keepdims=True)
            xn = (x - mu) / jnp.sqrt(var + 1e-05) * g + bln
            hg = xn @ W1 + b1
            a, gate = jnp.split(hg, 2, -1)
            return a * jax.nn.gelu(gate, approximate=False) @ W2 + b2
        key = jax.random.key(seed)
        ks = jax.random.split(key, 8)
        B, N = (2, 256)
        init = lambda k, shape: jax.random.normal(k, shape, jnp.float32) * 0.02
        return {'x': jax.random.normal(ks[0], (B, N, DIM), jnp.float32), 'Wqkv': init(ks[1], (DEPTH, DIM, 3 * INNER)), 'q_scale': jnp.ones((DEPTH, DIM_HEAD), jnp.float32), 'k_scale': jnp.ones((DEPTH, DIM_HEAD), jnp.float32), 'Wo': init(ks[2], (DEPTH, INNER, DIM)), 'ln_g': jnp.ones((DEPTH, DIM), jnp.float32), 'ln_b': jnp.zeros((DEPTH, DIM), jnp.float32), 'W1': init(ks[3], (DEPTH, DIM, 2 * DIM_INNER)), 'b1': jnp.zeros((DEPTH, 2 * DIM_INNER), jnp.float32), 'W2': init(ks[4], (DEPTH, DIM_INNER, DIM)), 'b2': jnp.zeros((DEPTH, DIM), jnp.float32)}
    _L0_ffn_in = _L0_ffn_setup()
    _d = {'L0_attn_x': _L0_attn_in['x'], 'L0_attn_Wqkv_w': _L0_attn_in['Wqkv_w'], 'L0_attn_Wqkv_b': _L0_attn_in['Wqkv_b'], 'L0_attn_gn_w': _L0_attn_in['gn_w'], 'L0_attn_gn_b': _L0_attn_in['gn_b'], 'L0_attn_out_w': _L0_attn_in['out_w'], 'L0_attn_out_b': _L0_attn_in['out_b'], 'L0_ffn_Wqkv': _L0_ffn_in['Wqkv'], 'L0_ffn_q_scale': _L0_ffn_in['q_scale'], 'L0_ffn_k_scale': _L0_ffn_in['k_scale'], 'L0_ffn_Wo': _L0_ffn_in['Wo'], 'L0_ffn_ln_g': _L0_ffn_in['ln_g'], 'L0_ffn_ln_b': _L0_ffn_in['ln_b'], 'L0_ffn_W1': _L0_ffn_in['W1'], 'L0_ffn_b1': _L0_ffn_in['b1'], 'L0_ffn_W2': _L0_ffn_in['W2'], 'L0_ffn_b2': _L0_ffn_in['b2']}
    _x0 = _d['L0_attn_x']
    _d['L0_attn_x'] = jax.random.normal(jax.random.fold_in(jax.random.key(seed), 1), (4, 1024, 128), dtype=_x0.dtype)
    del _x0
    return _d

def reference(L0_attn_x, L0_attn_Wqkv_w, L0_attn_Wqkv_b, L0_attn_gn_w, L0_attn_gn_b, L0_attn_out_w, L0_attn_out_b, L0_ffn_Wqkv, L0_ffn_q_scale, L0_ffn_k_scale, L0_ffn_Wo, L0_ffn_ln_g, L0_ffn_ln_b, L0_ffn_W1, L0_ffn_b1, L0_ffn_W2, L0_ffn_b2):

    def _L0_attn_ref(x, Wqkv_w, Wqkv_b, gn_w, gn_b, out_w, out_b):
        import jax, jax.numpy as jnp
        import numpy as np
        D_MODEL = 128
        N_HEADS = 32
        HEAD_DIM = D_MODEL // N_HEADS
        EPS = 1e-05
        B, S, Dm = x.shape
        H, Dh = (N_HEADS, HEAD_DIM)
        qkv = x @ Wqkv_w.T + Wqkv_b
        qkv = qkv.reshape(B, S, 3, H, Dh)
        q, k, v = (qkv[:, :, 0], qkv[:, :, 1], qkv[:, :, 2])
        a = jnp.einsum('bthd,bshd->bhts', q, k)
        ctx = jnp.einsum('bhts,bshd->bthd', a, v)
        g = ctx.transpose(0, 2, 3, 1)
        mean = g.mean(axis=(2, 3), keepdims=True)
        var = ((g - mean) ** 2).mean(axis=(2, 3), keepdims=True)
        gh = (g - mean) * jax.lax.rsqrt(var + EPS)
        gh = gh * gn_w.reshape(H, Dh, 1) + gn_b.reshape(H, Dh, 1)
        ctx = gh.transpose(0, 3, 1, 2).reshape(B, S, Dm)
        return ctx @ out_w.T + out_b

    def _L0_ffn_ref(x, Wqkv, q_scale, k_scale, Wo, ln_g, ln_b, W1, b1, W2, b2):
        import jax, jax.numpy as jnp
        import numpy as np
        DIM = 128
        DEPTH = 6
        HEADS = 16
        DIM_HEAD = 64
        WINDOW = 32
        INNER = HEADS * DIM_HEAD
        DIM_INNER = int(DIM * 4 * 2 / 3)
        QK_SCALE = 8.0

        def shift_tokens(t):
            a, s = jnp.split(t, 2, -1)
            s = jnp.pad(s, ((0, 0), (1, 0), (0, 0)))[:, :-1]
            return jnp.concatenate([a, s], -1)

        def l2norm(t):
            return t / jnp.maximum(jnp.linalg.norm(t, axis=-1, keepdims=True), 1e-12)

        def rotate_half(x):
            x1, x2 = jnp.split(x, 2, -1)
            return jnp.concatenate([-x2, x1], -1)

        def rotary_tables(n):
            half = jnp.arange(0, DIM_HEAD, 2, dtype=jnp.float32)
            inv_freq = 1.0 / 10000.0 ** (half / DIM_HEAD)
            t = jnp.arange(n, dtype=jnp.float32)
            freqs = t[:, None] * inv_freq[None, :]
            freqs = jnp.concatenate([freqs, freqs], -1)
            base_scale = (half + 0.4 * DIM_HEAD) / (1.4 * DIM_HEAD)
            power = (t - n // 2) / (WINDOW // 2)
            scale = base_scale[None, :] ** power[:, None]
            scale = jnp.concatenate([scale, scale], -1)
            return (freqs, scale)

        def local_attention(q, k, v):
            b, h, n, d = q.shape
            w = WINDOW
            nw = n // w
            bq = q.reshape(b, h, nw, w, d)
            bk = k.reshape(b, h, nw, w, d)
            bv = v.reshape(b, h, nw, w, d)

            def look(t):
                p = jnp.pad(t, ((0, 0), (0, 0), (1, 0), (0, 0), (0, 0)))
                return jnp.concatenate([p[:, :, :nw], p[:, :, 1:]], axis=3)
            bk2, bv2 = (look(bk), look(bv))
            seq = jnp.arange(n).reshape(nw, w)
            seq_p = jnp.pad(seq, ((1, 0), (0, 0)), constant_values=-1)
            jt = jnp.concatenate([seq_p[:nw], seq_p[1:]], axis=1)
            it = seq[:, :, None]
            jb = jt[:, None, :]
            mask = (it < jb) | (it > jb + w) | (jb == -1)
            sim = jnp.einsum('bhwie,bhwje->bhwij', bq, bk2) * QK_SCALE
            sim = jnp.where(mask, -jnp.finfo(sim.dtype).max, sim)
            attn = jax.nn.softmax(sim, -1)
            out = jnp.einsum('bhwij,bhwje->bhwie', attn, bv2)
            return out.reshape(b, h, n, d)

        def attn_layer(x, Wqkv, qs, ksc, Wo):
            b, n, _ = x.shape
            qkv = x @ Wqkv
            q, k, v = jnp.split(qkv, 3, -1)
            sh = lambda t: t.reshape(b, n, HEADS, DIM_HEAD).transpose(0, 2, 1, 3)
            q, k, v = (sh(q), sh(k), sh(v))
            q = l2norm(q) * qs
            k = l2norm(k) * ksc
            freqs, scale = rotary_tables(n)
            cos, sin = (jnp.cos(freqs), jnp.sin(freqs))
            q = q * cos * scale + rotate_half(q) * sin * scale
            inv = 1.0 / scale
            k = k * cos * inv + rotate_half(k) * sin * inv
            out = local_attention(q, k, v)
            out = out.transpose(0, 2, 1, 3).reshape(b, n, INNER)
            return out @ Wo

        def ffn_layer(x, g, bln, W1, b1, W2, b2):
            mu = x.mean(-1, keepdims=True)
            var = ((x - mu) ** 2).mean(-1, keepdims=True)
            xn = (x - mu) / jnp.sqrt(var + 1e-05) * g + bln
            hg = xn @ W1 + b1
            a, gate = jnp.split(hg, 2, -1)
            return a * jax.nn.gelu(gate, approximate=False) @ W2 + b2
        for i in range(DEPTH):
            x = attn_layer(shift_tokens(x), Wqkv[i], q_scale[i], k_scale[i], Wo[i]) + x
            x = ffn_layer(shift_tokens(x), ln_g[i], ln_b[i], W1[i], b1[i], W2[i], b2[i]) + x
        return x
    x = L0_attn_x
    x = x + _layernorm(_L0_attn_ref(_layernorm(x, axis=-1), L0_attn_Wqkv_w, L0_attn_Wqkv_b, L0_attn_gn_w, L0_attn_gn_b, L0_attn_out_w, L0_attn_out_b), axis=-1)
    x = x + _layernorm(_L0_ffn_ref(_layernorm(x, axis=-1), L0_ffn_Wqkv, L0_ffn_q_scale, L0_ffn_k_scale, L0_ffn_Wo, L0_ffn_ln_g, L0_ffn_ln_b, L0_ffn_W1, L0_ffn_b1, L0_ffn_W2, L0_ffn_b2), axis=-1)
    return x

_drawn_inputs = setup_inputs


def setup_inputs(seed=0):
    import zlib

    import numpy as np

    out = dict(_drawn_inputs(seed))
    spreads = {'L0_attn_gn_w': (1.0, 0.2),
     'L0_attn_gn_b': (0.0, 0.1),
     'L0_ffn_q_scale': (1.0, 0.6),
     'L0_ffn_k_scale': (1.0, 0.6),
     'L0_ffn_ln_g': (1.0, 0.6),
     'L0_ffn_ln_b': (0.0, 0.8),
     'L0_ffn_b1': (0.0, 0.8),
     'L0_ffn_b2': (0.0, 0.328)}
    factors = {'L0_attn_Wqkv_b': 8.0, 'L0_attn_out_b': 7.665, 'L0_ffn_W1': 4.499, 'L0_ffn_W2': 4.428}
    for name, (base, spread) in spreads.items():
        noise = np.random.default_rng([zlib.crc32(name.encode()), seed]).standard_normal(out[name].shape)
        drawn = base * np.exp(spread * noise) if base else spread * noise
        out[name] = jnp.asarray(drawn.astype(out[name].dtype))
    for name, factor in factors.items():
        out[name] = (out[name] * factor).astype(out[name].dtype)
    return out
```

```python
from contextlib import ExitStack

import numpy as np

import concourse.bass as bass
from concourse import mybir

F32 = mybir.dt.float32
ALU = mybir.AluOpType
ACT = mybir.ActivationFunctionType
AX = mybir.AxisListType

B, S, D = 4, 1024, 128
P = 128
TPB = S // P
TILES = B * TPB
DEPTH = 6
HEADS, DH, WIN = 16, 64, 32
INNER = HEADS * DH
HALF = DH // 2
QUADS = 4
QH = HEADS // QUADS
QC = QH * DH
UNITS = TILES * QUADS
GQ = P // 2
GK = GQ + WIN
KW = WIN + P
HID = int(D * 4 * 2 / 3)
HCH = [(c, min(128, HID - c)) for c in range(0, HID, 128)]
XB = WIN + S + WIN
FT = 512
A_HEAD = 4
EPS = 1e-5
MASKED = -1e30


def kernel_program(nc, x, wkv_t, bkv, wq_t, bq, gn_w, gn_b, wo_t, bo,
                   Wqkv, q_scale, k_scale, Wo, ln_g, ln_b, W1, b1, W2, b2,
                   rotary, band, ident_in, block_in, keep_in, out):
    with ExitStack() as ctx:
        def sb(name, shape):
            return ctx.enter_context(nc.sbuf_tensor(name, shape, F32))

        def sem(name):
            return ctx.enter_context(nc.semaphore(name))

        bank = [ctx.enter_context(nc.psum_tensor(f"bank{i}", [P, 512], F32)) for i in range(8)]

        X = sb("X", [P, B * XB])
        Y = sb("Y", [P, B * XB])
        resid = sb("resid", [P, TILES, D])
        ident = sb("ident", [P, P])
        block = sb("block", [P, 2, P])
        ones = sb("ones", [P, P])
        half_neg = sb("half_neg", [P, 2 * QH])

        wkv_sb = sb("wkv_sb", [P, 2 * D])
        wq_sb = sb("wq_sb", [P, D])
        wout_sb = sb("wout_sb", [P, D])
        bkv_sb = sb("bkv_sb", [P, 2 * D])
        bo_sb = sb("bo_sb", [P, D])
        cols = sb("cols", [P, 3])
        xn = sb("xn", [P, TPB, D])
        xc = sb("xc", [P, TPB, D])
        sq = sb("sq", [P, TPB, D])
        xnT = sb("xnT", [P, S])
        kv = sb("kv", [P, TPB, 2 * D])
        state = sb("state", [P, P])
        qT = sb("qT", [P, S])
        ctxT = sb("ctxT", [P, S])
        stat = sb("stat", [P, 5, TPB])
        csum = sb("csum", [P, 3])
        cssq = sb("cssq", [P, 3])
        gstat = sb("gstat", [P, 5])

        wqk = sb("wqk", [P, QUADS, 2, QC])
        wv = sb("wv", [P, INNER])
        wo = sb("wo", [P, INNER // P, D])
        scales = sb("scales", [P, 2, DH])
        tables = sb("tables", [P, TPB, 2, 2, DH])
        rotary_sb = sb("rotary_sb", [P, TPB, 2, 2, DH])
        w1 = sb("w1", [P, 2 * HID])
        w2 = sb("w2", [P, len(HCH), D])
        fcols = sb("fcols", [P, 3 + 2 * len(HCH)])

        xw = sb("xw", [P, KW])
        masks = sb("masks", [P, TPB, GK])
        mask = sb("mask", [P, GK])
        keep = sb("keep", [P, TPB])
        square = sb("square", [P, 2 * QH, DH])
        sumsq = sb("sumsq", [P, 2, 2, 2 * QH])
        rnorm = sb("rnorm", [P, QUADS, 2 * QH])
        knorm = sb("knorm", [P, 2, QH, DH])
        rot = sb("rot", [P, 2, 2, 2, QH, DH])
        qk = sb("qk", [P, QUADS, 4, KW])
        vs = sb("vs", [GK, QUADS, 2, QC])
        scores = sb("scores", [P, QH, GK])
        probs = sb("probs", [P, QH, GK])
        rowmax = sb("rowmax", [P, QH])
        nbias = sb("nbias", [P, QH])
        rowsum = sb("rowsum", [P, QH])
        rsum = sb("rsum", [P, QH])
        pT = sb("pT", [GK, QH * P])
        oT = sb("oT", [P, 2, 2 * P])

        fxc = sb("fxc", [P, 2, FT])
        fsq = sb("fsq", [P, 2, FT])
        fvar = sb("fvar", [P, 2, FT // P])
        frs = sb("frs", [P, 2, FT // P])
        fdiag = sb("fdiag", [P, 2, FT])
        one = sb("one", [P, P])
        fxn = sb("fxn", [P, 2, FT])
        gate = sb("gate", [P, 2, FT])
        hidden = sb("hidden", [P, 2, len(HCH), FT])

        def sems(names):
            return [sem(name) for name in names.split()]

        consts_in, x_in, consts_set, out_stored = sems("consts_in x_in consts_set out_stored")
        attn_in, ffn_in, tables_set = sems("attn_in ffn_in tables_set")
        ln_step, ln_rsqrt = sems("ln_step ln_rsqrt")
        (a_xn, a_xnT_ps, a_xnT, a_kv_ps, a_kv, a_state_ps, a_state, a_q_ps, a_q, a_ctx_ps, a_ctx) = sems(
            "a_xn a_xnT_ps a_xnT a_kv_ps a_kv a_state_ps a_state a_q_ps a_q a_ctx_ps a_ctx")
        (a_csum, a_mean_ps, a_mean, a_sq, a_ssq, a_var_ps, a_var, a_rs, a_scale, a_shift, a_gn) = sems(
            "a_csum a_mean_ps a_mean a_sq a_ssq a_var_ps a_var a_rs a_scale a_shift a_gn")
        (a_out_ps, a_out, a_ln2, a_x1, a_xn2, a_xn2T_ps, x_ready) = sems(
            "a_out_ps a_out a_ln2 a_x1 a_xn2 a_xn2T_ps x_ready")
        z_xT, z_x_ps, z_x, z_ln, z_out = sems("z_xT z_x_ps z_x z_ln z_out")
        proj_done, v_done, qkT_done, s_done, pT_done, o_done = sems("proj_done v_done qkT_done s_done pT_done o_done")
        square_done, v_kept, qk_kept, exp_done, o_kept = sems("square_done v_kept qk_kept exp_done o_kept")
        qrot_done, ssq_done, floor_done, kn_done = sems("qrot_done ssq_done floor_done kn_done")
        max_done, nbias_done, rsum_done, pT_kept = sems("max_done nbias_done rsum_done pT_kept")
        rnorm_done, krot_done, probs_done, tail_moved = sems("rnorm_done krot_done probs_done tail_moved")
        xw_ready, mask_ready, y_done, y_written = sems("xw_ready mask_ready y_done y_written")
        mean_done, center_done, fsq_done, var_done, eps_done, frs_done, fn_done, faff_done = sems(
            "mean_done center_done fsq_done var_done eps_done frs_done fn_done faff_done")
        fdiag_done, spread_done = sems("fdiag_done spread_done")
        up_done, gelu_done, hid_done, down_done = sems("up_done gelu_done hid_done down_done")

        NCONST, NATTN, NFFN = 13, 6, 6 + 2 * len(HCH)
        NSET = 6

        def start_at_one(eng, names):
            for s in names:
                eng.sem_inc(s, 1)

        CH = len(HCH)
        blk = ctx.enter_context(nc.Block())

        def column(tile):
            return tile * P + (tile // TPB) * (XB - S)

        def alone(eng):
            eng.nop(nofuse=True)

        def on(n, lag):
            return n is None or 0 <= n - lag < UNITS

        def pipeline(eng, slot):
            for j in range(QUADS):
                slot(j, 0, j)
            with eng.Fori(1, TILES) as t:
                for j in range(QUADS):
                    slot(j, t, None)
            for j in range(QUADS):
                slot(j, TILES, UNITS + j)

        def tiles_of(b):
            return resid[:, bass.ds(b * TPB, TPB), :]

        def by_tile(ap):
            return ap.rearrange("p (t n) -> p t n", n=D)

        def over_d(col, n):
            return col[:, :, None].broadcast_to([P, n, D])

        def rotate(eng, cos_part, sin_part, src, tab):
            eng.tensor_tensor(cos_part, src, tab[:, 0, None, :].broadcast_to([P, QH, DH]), ALU.mult)
            swapped = bass.AP(sin_part.tensor, sin_part.offset + HALF,
                              [list(sin_part.ap[0]), [DH, QH], [-HALF, 2], [1, HALF]])
            return eng.tensor_tensor(
                swapped, src.rearrange("p h (a e) -> p h a e", a=2),
                tab[:, 1, :].rearrange("p (a e) -> p a e", a=2)[:, None, :, :].broadcast_to([P, QH, 2, HALF]),
                ALU.mult)

        @blk.sync
        def _(sp):
            def row(v, n):
                return v.rearrange("(a n) -> a n", a=1).broadcast_to([P, n])

            def col(v):
                return v.rearrange("(n a) -> n a", a=1)

            start_at_one(sp, (out_stored,))
            for b in range(B):
                sp.dma_start(tiles_of(b), x[b].rearrange("(n p) d -> p n d", p=P)).then_inc(x_in, 16)
            for dst, src in (
                (ident[:], ident_in), (block[:], block_in), (wkv_sb[:], wkv_t), (wq_sb[:], wq_t),
                (wout_sb[:], wo_t), (bkv_sb[:], row(bkv, 2 * D)), (bo_sb[:], row(bo, D)),
                (cols[:, 0:1], col(bq)), (cols[:, 1:2], col(gn_w)), (cols[:, 2:3], col(gn_b)),
                (rotary_sb[:], rotary), (masks[:], band), (keep[:], keep_in),
            ):
                sp.dma_start(dst, src).then_inc(consts_in, 16)
            with sp.Fori(0, DEPTH) as l:
                sp.wait_ge(y_written, l * TILES + 1)
                for dst, src in (
                    (wqk[:, :, 0, :], Wqkv[l, :, 0:INNER].rearrange("p (j n) -> p j n", j=QUADS)),
                    (wqk[:, :, 1, :], Wqkv[l, :, INNER:2 * INNER].rearrange("p (j n) -> p j n", j=QUADS)),
                    (wv[:], Wqkv[l, :, 2 * INNER:3 * INNER]),
                    (wo[:], Wo[l].rearrange("(c p) n -> p c n", p=P)),
                    (scales[:, 0, :], q_scale[l].rearrange("(a n) -> a n", a=1).broadcast_to([P, DH])),
                    (scales[:, 1, :], k_scale[l].rearrange("(a n) -> a n", a=1).broadcast_to([P, DH])),
                ):
                    sp.dma_start(dst, src).then_inc(attn_in, 16)
                sp.wait_ge(x_ready, (l + 1) * 2 * B + 1)
                for dst, src in (
                    (w1[:], W1[l]),
                    (w2[:, 0:CH - 1, :], W2[l, 0:(CH - 1) * P, :].rearrange("(c p) n -> p c n", p=P)),
                    (w2[0:HCH[-1][1], CH - 1, :], W2[l, (CH - 1) * P:HID, :]),
                    (fcols[:, 0:1], col(ln_g[l])), (fcols[:, 1:2], col(ln_b[l])), (fcols[:, 2:3], col(b2[l])),
                ):
                    sp.dma_start(dst, src).then_inc(ffn_in, 16)
                for side in range(2):
                    for c, (c0, cn) in enumerate(HCH):
                        k = 3 + side * CH + c
                        sp.dma_start(fcols[0:cn, k:k + 1],
                                     col(b1[l, side * HID + c0:side * HID + c0 + cn])).then_inc(ffn_in, 16)
            with sp.Fori(0, B) as b:
                sp.wait_ge(z_out, b + 1)
                sp.dma_start(out[b].rearrange("(n p) d -> p n d", p=P), xn[:]).then_inc(out_stored, 16)
            sp.wait_ge(out_stored, B * 16 + 1)

        @blk.vector
        def _(dve):
            def ln_stats(src, call):
                done = call * 6
                dve.tensor_reduce(stat[:, 0, :], src, AX.X, ALU.add).then_inc(ln_step, 1)
                dve.wait_ge(ln_step, done + 1)
                dve.tensor_scalar(stat[:, 1, :], stat[:, 0, :], -1.0 / D, None, ALU.mult).then_inc(ln_step, 1)
                dve.wait_ge(ln_step, done + 2)
                dve.tensor_tensor(xc[:], src, over_d(stat[:, 1, :], TPB), ALU.add).then_inc(ln_step, 1)
                dve.wait_ge(ln_step, done + 3)
                dve.tensor_tensor(sq[:], xc[:], xc[:], ALU.mult).then_inc(ln_step, 1)
                dve.wait_ge(ln_step, done + 4)
                dve.tensor_reduce(stat[:, 2, :], sq[:], AX.X, ALU.add).then_inc(ln_step, 1)
                dve.wait_ge(ln_step, done + 5)
                dve.tensor_scalar(stat[:, 3, :], stat[:, 2, :], 1.0 / D, EPS, ALU.mult, ALU.add).then_inc(ln_step, 1)

            def ln_scale(dst, call):
                dve.wait_ge(ln_rsqrt, call + 1)
                return dve.tensor_tensor(dst, xc[:], over_d(stat[:, 4, :], TPB), ALU.mult)

            start_at_one(dve, (qrot_done, ssq_done, floor_done, kn_done, max_done, nbias_done, rsum_done,
                               pT_kept, y_written, z_x))
            dve.memset(ones[:], 1.0 / D).then_inc(consts_set, 1)
            dve.memset(one[:], 1.0).then_inc(consts_set, 1)
            dve.memset(half_neg[:], -0.5).then_inc(consts_set, 1)
            dve.memset(X[:], 0.0).then_inc(consts_set, 1)
            dve.memset(Y[:], 0.0).then_inc(consts_set, 1)
            dve.memset(qk[:], 0.0).then_inc(consts_set, 1)
            dve.wait_ge(consts_in, NCONST * 16)
            dve.wait_ge(x_in, B * 16)

            with dve.Fori(0, B) as b:
                ln_stats(tiles_of(b), b * 3)
                dve.wait_ge(a_xn2T_ps, b * 2 + 1)
                ln_scale(xn[:], b * 3).then_inc(a_xn, 1)
                for i in range(4):
                    dve.wait_ge(a_kv_ps, b * 4 + i + 1)
                    dve.tensor_tensor(kv[:, 2 * i:2 * i + 2, :],
                                      bank[2 + i][:].rearrange("p (t n) -> p t n", t=2),
                                      bkv_sb[:, None, :].broadcast_to([P, 2, 2 * D]), ALU.add).then_inc(a_kv, 1)
                dve.wait_ge(a_state_ps, b + 1)
                dve.tensor_tensor(state[:], bank[6][:, 0:P], block[:, 0, :], ALU.mult).then_inc(a_state, 1)
                dve.wait_ge(a_ctx, b * 2 + 2)
                dve.tensor_tensor(csum[:, 2:3], csum[:, 0:1], csum[:, 1:2], ALU.add).then_inc(a_csum, 1)
                dve.wait_ge(a_mean_ps, b + 1)
                dve.tensor_scalar(gstat[:, 0:1], bank[7][:, 0:1], -1.0, None, ALU.mult).then_inc(a_mean, 1)
                dve.wait_ge(a_sq, b * 2 + 2)
                dve.tensor_tensor(cssq[:, 2:3], cssq[:, 0:1], cssq[:, 1:2], ALU.add).then_inc(a_ssq, 1)
                dve.wait_ge(a_var_ps, b + 1)
                dve.tensor_scalar(gstat[:, 1:2], bank[7][:, 0:1], EPS, None, ALU.add).then_inc(a_var, 1)
                dve.wait_ge(a_rs, b + 1)
                dve.tensor_tensor(gstat[:, 3:4], gstat[:, 2:3], cols[:, 1:2], ALU.mult).then_inc(a_scale, 1)
                dve.wait_ge(a_scale, b + 1)
                dve.scalar_tensor_tensor(out=gstat[:, 4:5], in0=gstat[:, 3:4], scalar=gstat[:, 0:1],
                                         in1=cols[:, 2:3], op0=ALU.mult, op1=ALU.add).then_inc(a_shift, 1)
                for h in range(2):
                    dve.wait_ge(a_out_ps, b * 2 + h + 1)
                    dve.tensor_tensor(xn[:, 4 * h:4 * h + 4, :], by_tile(bank[4 + h][:]),
                                      bo_sb[:, None, :].broadcast_to([P, 4, D]), ALU.add).then_inc(a_out, 1)
                dve.wait_ge(a_out, b * 2 + 2)
                ln_stats(xn[:], b * 3 + 1)
                ln_scale(sq[:], b * 3 + 1).then_inc(a_ln2, 1)
                dve.wait_ge(a_ln2, b + 1)
                dve.tensor_tensor(tiles_of(b), tiles_of(b), sq[:], ALU.add).then_inc(a_x1, 1)
                dve.wait_ge(a_x1, b + 1)
                alone(dve)
                ln_stats(tiles_of(b), b * 3 + 2)
                ln_scale(xn[:], b * 3 + 2).then_inc(a_xn2, 1)

            with dve.Fori(0, DEPTH) as l:
                dve.wait_ge(attn_in, (l + 1) * NATTN * 16)
                for side in range(2):
                    dve.tensor_tensor(tables[:, :, side, :, :], rotary_sb[:, :, side, :, :],
                                      scales[:, side, None, None, :].broadcast_to([P, TPB, 2, DH]),
                                      ALU.mult).then_inc(tables_set, 1)
                dve.wait_ge(tables_set, l * 2 + 2)

                def slot(j, t, n):
                    u = l * UNITS + t * QUADS + j + 1
                    r = j % 2
                    if on(n, 4) and j == 3:
                        c = column(t - 1) + WIN
                        dve.wait_ge(y_done, l * TILES + t + 1)
                        dve.tensor_tensor(Y[0:64, bass.ds(c, P)], bank[7][0:64, 0:P],
                                          X[0:64, bass.ds(c, P)], ALU.add)
                        dve.tensor_tensor(Y[64:128, bass.ds(c + 1, P)], bank[7][64:128, 0:P],
                                          X[64:128, bass.ds(c + 1, P)], ALU.add).then_inc(y_written, 1)
                    if on(n, 2):
                        dve.wait_ge(exp_done, u - 1)
                        dve.reciprocal(rsum[:], rowsum[:]).then_inc(rsum_done, 1)
                    if on(n, 0):
                        dve.wait_ge(square_done, u + 1)
                        rotate(dve, rot[:, r, 0, 0], rot[:, r, 0, 1],
                               bank[0][:, 0:QC].rearrange("p (h d) -> p h d", h=QH),
                               tables[:, bass.ds(t % TPB, 1), 0, :, :].rearrange("p a c d -> p (a c) d")
                               ).then_inc(qrot_done, 1)
                    if on(n, 0):
                        dve.tensor_reduce(sumsq[:, r, 0, :], square[:], AX.X, ALU.add).then_inc(ssq_done, 1)
                        dve.wait_ge(ssq_done, u + 1)
                        dve.tensor_scalar(sumsq[:, r, 1, :], sumsq[:, r, 0, :], 1e-24, None,
                                          ALU.max).then_inc(floor_done, 1)
                    if on(n, 2):
                        dve.wait_ge(pT_done, u - 1)
                        dve.tensor_copy(pT[:], bank[5][0:GK, :]).then_inc(pT_kept, 1)
                    if on(n, 0):
                        dve.wait_ge(rnorm_done, u + 1)
                        dve.tensor_tensor(knorm[:, r], bank[0][:, QC:2 * QC].rearrange("p (h d) -> p h d", h=QH),
                                          rnorm[:, j, QH:2 * QH, None].broadcast_to([P, QH, DH]),
                                          ALU.mult).then_inc(kn_done, 1)
                    if on(n, 1):
                        before = (j - 1) % QUADS
                        if before == 0:
                            dve.wait_ge(mask_ready, l * TILES + t + 2)
                        dve.wait_ge(s_done, u)
                        alone(dve)
                        for h in range(QH):
                            last = dve.tensor_tensor_reduce(
                                scores[:, h, :], bank[3 + h % 2][:, (h // 2) * GK:(h // 2 + 1) * GK], mask[:],
                                1.0, -3e38, ALU.add, ALU.max, rowmax[:, h:h + 1])
                        last.then_inc(max_done, 1)
                        dve.wait_ge(max_done, u)
                        dve.scalar_tensor_tensor(out=nbias[:], in0=rowmax[:], scalar=-1.0,
                                                 in1=rnorm[:, before, 0:QH], op0=ALU.mult,
                                                 op1=ALU.mult).then_inc(nbias_done, 1)

                pipeline(dve, slot)

                dve.wait_ge(ffn_in, (l + 1) * NFFN * 16)
                dve.wait_ge(y_written, (l + 1) * TILES + 1)
                alone(dve)
                with dve.Fori(0, B) as b:
                    v0 = l * 2 * B + b * 2
                    for h in range(2):
                        dve.wait_ge(mean_done, v0 + h + 1)
                        dve.tensor_tensor(fxc[:, h], Y[:, bass.ds(b * XB + WIN + h * FT, FT)], bank[h][:],
                                          ALU.subtract).then_inc(center_done, 1)
                    for h in range(2):
                        dve.wait_ge(var_done, v0 + h + 1)
                        dve.tensor_scalar(fvar[:, h], bank[h][:, 0:FT // P], EPS, None, ALU.add).then_inc(eps_done, 1)
                    for h in range(2):
                        dve.wait_ge(frs_done, v0 + h + 1)
                        dve.tensor_tensor(by_tile(fdiag[:, h]), ident[:, None, :].broadcast_to([P, FT // P, P]),
                                          over_d(frs[:, h], FT // P), ALU.mult).then_inc(fdiag_done, 1)
                    for h in range(2):
                        dve.wait_ge(spread_done, v0 + h + 1)
                        dve.tensor_tensor(fsq[:, h], fxc[:, h], bank[h][:], ALU.mult).then_inc(fn_done, 1)
                    for h in range(2):
                        c = b * XB + WIN + h * FT
                        for k, (c0, cn) in enumerate(HCH):
                            dve.wait_ge(gelu_done, (v0 + h) * CH + k + 1)
                            dve.scalar_tensor_tensor(out=hidden[0:cn, h, k, :], in0=bank[4 + (h + k) % 2][0:cn, :],
                                                     scalar=fcols[0:cn, 3 + k:4 + k],
                                                     in1=gate[0:cn, (h + k) % 2, :],
                                                     op0=ALU.add, op1=ALU.mult).then_inc(hid_done, 1)
                        dve.wait_ge(down_done, v0 + h + 1)
                        for side in range(2):
                            rows = slice(64 * side, 64 * side + 64)
                            last = dve.scalar_tensor_tensor(
                                out=X[rows, bass.ds(c + side, FT)], in0=bank[6 + h][rows, :],
                                scalar=fcols[rows, 2:3], in1=Y[rows, bass.ds(c + side, FT)],
                                op0=ALU.add, op1=ALU.add)
                        last.then_inc(x_ready, 1)

            with dve.Fori(0, B) as b:
                dve.wait_ge(out_stored, b * 16 + 1)
                dve.wait_ge(z_x_ps, b + 2)
                for h in range(2):
                    dve.tensor_copy(xn[:, 4 * h:4 * h + 4, :], by_tile(bank[h][:])).then_inc(z_x, 1)
                dve.wait_ge(z_x, b * 2 + 3)
                ln_stats(xn[:], b + 3 * B)
                ln_scale(sq[:], b + 3 * B).then_inc(z_ln, 1)
                dve.wait_ge(z_ln, b + 1)
                dve.tensor_tensor(xn[:], sq[:], tiles_of(b), ALU.add).then_inc(z_out, 1)

        @blk.gpsimd
        def _(pool):
            def ln_pow(call):
                pool.wait_ge(ln_step, call * 6 + 6)
                pool.tensor_tensor(stat[:, 4, :], stat[:, 3, :], half_neg[:, 0:TPB], ALU.pow).then_inc(ln_rsqrt, 1)

            start_at_one(pool, (rnorm_done, krot_done, probs_done, tail_moved, xw_ready, mask_ready))
            pool.wait_ge(consts_set, NSET)
            with pool.Fori(0, B) as b:
                ln_pow(b * 3)
                pool.wait_ge(a_var, b + 1)
                pool.tensor_tensor(gstat[:, 2:3], gstat[:, 1:2], half_neg[:, 0:1], ALU.pow).then_inc(a_rs, 1)
                ln_pow(b * 3 + 1)
                ln_pow(b * 3 + 2)

            with pool.Fori(0, DEPTH) as l:
                pool.wait_ge(x_ready, (l + 1) * 2 * B + 1)
                pool.wait_ge(tables_set, l * 2 + 2)

                def slot(j, t, n):
                    u = l * UNITS + t * QUADS + j + 1
                    r = j % 2
                    if on(n, 0) and j == 0:
                        pool.wait_ge(v_done, u)
                        alone(pool)
                        pool.tensor_copy(xw[:], X[:, bass.ds(column(t), KW)]).then_inc(xw_ready, 1)
                    if on(n, 0):
                        if n is None:
                            pool.wait_ge(s_done, u - 3)
                            alone(pool)
                        pool.tensor_tensor(qk[:, j, 2:4, 0:WIN], qk[:, j, 2:4, P:KW],
                                           keep[:, bass.ds(t % TPB, 1), None].broadcast_to([P, 2, WIN]),
                                           ALU.mult).then_inc(tail_moved, 1)
                    if on(n, 2):
                        pool.wait_ge(rsum_done, u - 1)
                        pool.tensor_tensor(probs[:], probs[:], rsum[:, :, None].broadcast_to([P, QH, GK]),
                                           ALU.mult).then_inc(probs_done, 1)
                    if on(n, 0):
                        pool.wait_ge(floor_done, u + 1)
                        pool.tensor_tensor(rnorm[:, j, :], sumsq[:, r, 1, :], half_neg[:, 0:2 * QH],
                                           ALU.pow).then_inc(rnorm_done, 1)
                    if on(n, 0) and j == 1:
                        pool.wait_ge(max_done, u - 1)
                        alone(pool)
                        pool.tensor_copy(mask[:], masks[:, bass.ds(t % TPB, 1), :].rearrange(
                            "p a k -> p (a k)")).then_inc(mask_ready, 1)
                    if on(n, 0):
                        pool.wait_ge(kn_done, u + 1)
                        alone(pool)
                        rotate(pool, rot[:, r, 1, 0], rot[:, r, 1, 1], knorm[:, r],
                               tables[:, bass.ds(t % TPB, 1), 1, :, :].rearrange("p a c d -> p (a c) d")
                               ).then_inc(krot_done, 1)

                pipeline(pool, slot)

                with pool.Fori(0, B) as b:
                    for h in range(2):
                        pool.wait_ge(eps_done, l * 2 * B + b * 2 + h + 1)
                        pool.tensor_tensor(frs[:, h], fvar[:, h], half_neg[:, 0:FT // P], ALU.pow).then_inc(frs_done, 1)

            with pool.Fori(0, B) as b:
                ln_pow(b + 3 * B)

        @blk.scalar
        def _(act):
            start_at_one(act, (square_done, v_kept, qk_kept, exp_done, o_kept, x_ready))
            act.wait_ge(consts_in, NCONST * 16)
            act.wait_ge(consts_set, NSET)
            with act.Fori(0, B) as b:
                for h in range(2):
                    act.wait_ge(a_xnT_ps, b * 2 + h + 1)
                    act.activation(xnT[:, 512 * h:512 * h + 512], bank[h][:], ACT.Copy).then_inc(a_xnT, 1)
                act.wait_ge(a_q_ps, b + 1)
                for h in range(2):
                    act.activation(qT[:, 512 * h:512 * h + 512], bank[h][:], ACT.Identity,
                                   bias=cols[:, 0:1]).then_inc(a_q, 1)
                act.wait_ge(a_ctx_ps, b + 1)
                for h in range(2):
                    act.activation(ctxT[:, 512 * h:512 * h + 512], bank[2 + h][:], ACT.Copy,
                                   accum_out=csum[:, h:h + 1]).then_inc(a_ctx, 1)
                act.wait_ge(a_mean, b + 1)
                act.wait_ge(a_ctx, b * 2 + 2)
                for h in range(2):
                    act.activation(xnT[:, 512 * h:512 * h + 512], ctxT[:, 512 * h:512 * h + 512], ACT.Square,
                                   bias=gstat[:, 0:1], accum_out=cssq[:, h:h + 1]).then_inc(a_sq, 1)
                act.wait_ge(a_shift, b + 1)
                for h in range(2):
                    act.activation(qT[:, 512 * h:512 * h + 512], ctxT[:, 512 * h:512 * h + 512], ACT.Identity,
                                   scale=gstat[:, 3:4], bias=gstat[:, 4:5]).then_inc(a_gn, 1)
                for h in range(2):
                    act.wait_ge(a_xn2T_ps, b * 2 + h + 2)
                    for side in range(2):
                        rows = slice(64 * side, 64 * side + 64)
                        last = act.activation(X[rows, bass.ds(b * XB + WIN + h * 512 + side, 512)],
                                              bank[h][rows, :], ACT.Copy)
                    last.then_inc(x_ready, 1)

            with act.Fori(0, DEPTH) as l:
                def slot(j, t, n):
                    u = l * UNITS + t * QUADS + j + 1
                    if on(n, 2):
                        two = (j - 2) % QUADS
                        act.wait_ge(nbias_done, u - 1)
                        for h in range(QH):
                            last = act.activation(probs[:, h, :], scores[:, h, :], ACT.Exp, bias=nbias[:, h:h + 1],
                                                  scale=rnorm[:, two, h:h + 1], accum_out=rowsum[:, h:h + 1])
                        last.then_inc(exp_done, 1)
                    if on(n, 0):
                        act.wait_ge(ssq_done, u)
                        act.wait_ge(proj_done, u + 1)
                        act.activation(square[:].rearrange("p h d -> p (h d)"), bank[0][:],
                                       ACT.Square).then_inc(square_done, 1)
                        act.wait_ge(v_done, u + 1)
                        act.activation(vs[:, j].rearrange("p g c -> p (g c)"), bank[1][0:GK, :],
                                       ACT.Copy).then_inc(v_kept, 1)
                    if on(n, 1):
                        before = (j - 1) % QUADS
                        act.wait_ge(tail_moved, u)
                        act.wait_ge(qkT_done, u)
                        act.activation(qk[:, before, :, WIN:KW], bank[2][:].rearrange("p (c k) -> p c k", c=4),
                                       ACT.Copy).then_inc(qk_kept, 1)
                    if on(n, 2):
                        act.wait_ge(o_done, u - 1)
                        act.activation(oT[:, j % 2, :], bank[6][:, 0:2 * P], ACT.Copy).then_inc(o_kept, 1)

                pipeline(act, slot)

                act.wait_ge(ffn_in, (l + 1) * NFFN * 16)
                with act.Fori(0, B) as b:
                    v0 = l * 2 * B + b * 2
                    for h in range(2):
                        act.wait_ge(center_done, v0 + h + 1)
                        act.activation(fsq[:, h], fxc[:, h], ACT.Square).then_inc(fsq_done, 1)
                    for h in range(2):
                        act.wait_ge(fn_done, v0 + h + 1)
                        act.activation(fxn[:, h], fsq[:, h], ACT.Identity, scale=fcols[:, 0:1],
                                       bias=fcols[:, 1:2]).then_inc(faff_done, 1)
                    for h in range(2):
                        for k, (c0, cn) in enumerate(HCH):
                            act.wait_ge(up_done, (v0 + h) * CH + k + 1)
                            act.activation(gate[0:cn, (h + k) % 2, :], bank[2 + (h + k) % 2][0:cn, :], ACT.Gelu,
                                           bias=fcols[0:cn, 3 + CH + k:4 + CH + k]).then_inc(gelu_done, 1)

            with act.Fori(0, B) as b:
                act.wait_ge(x_ready, (DEPTH + 1) * 2 * B + 1)
                act.wait_ge(z_x_ps, b + 1)
                for side in range(2):
                    rows = slice(64 * side, 64 * side + 64)
                    last = act.activation(ctxT[rows, :], X[rows, bass.ds(b * XB + WIN + side, S)], ACT.Copy)
                last.then_inc(z_xT, 1)

        @blk.tensor
        def _(pe):
            start_at_one(pe, (proj_done, v_done, qkT_done, s_done, pT_done, o_done, y_done, a_xn2T_ps, z_x_ps))
            pe.wait_ge(consts_in, NCONST * 16)
            pe.wait_ge(consts_set, NSET)

            def transposes(src, done):
                for h in range(2):
                    for i in range(4):
                        last = pe.transpose(bank[h][:, i * P:i * P + P], src(4 * h + i), ident[:])
                    last.then_inc(done, 1)

            with pe.Fori(0, B) as b:
                pe.wait_ge(x_ready, b * 2 + 1)
                pe.wait_ge(a_xn, b + 1)
                transposes(lambda i: xn[:, i, :], a_xnT_ps)
                for i in range(TPB):
                    if i % 4 == 0:
                        pe.wait_ge(a_xnT, b * 2 + i // 4 + 1)
                    last = pe.matmul(bank[2 + i // 2][:, (i % 2) * 2 * D:(i % 2 + 1) * 2 * D],
                                     xnT[:, i * P:i * P + P], wkv_sb[:], start=True, stop=True)
                    if i % 2:
                        last.then_inc(a_kv_ps, 1)
                for h in range(2):
                    last = pe.matmul(bank[h][:], wq_sb[:], xnT[:, 512 * h:512 * h + 512], start=True, stop=True)
                last.then_inc(a_q_ps, 1)
                for i in range(TPB):
                    if i % 2 == 0:
                        pe.wait_ge(a_kv, b * 4 + i // 2 + 1)
                    last = pe.matmul(bank[6][:, 0:P], kv[:, i, 0:D], kv[:, i, D:2 * D],
                                     start=(i == 0), stop=(i == TPB - 1))
                last.then_inc(a_state_ps, 1)
                pe.wait_ge(a_q, b * 2 + 2)
                pe.wait_ge(a_state, b + 1)
                for h in range(2):
                    last = pe.matmul(bank[2 + h][:], state[:], qT[:, 512 * h:512 * h + 512], start=True, stop=True)
                last.then_inc(a_ctx_ps, 1)
                pe.wait_ge(a_csum, b + 1)
                pe.matmul(bank[7][:, 0:1], block[:, 1, :], csum[:, 2:3], start=True, stop=True).then_inc(a_mean_ps, 1)
                pe.wait_ge(a_mean, b + 1)
                pe.wait_ge(a_ssq, b + 1)
                pe.matmul(bank[7][:, 0:1], block[:, 1, :], cssq[:, 2:3], start=True, stop=True).then_inc(a_var_ps, 1)
                pe.wait_ge(a_gn, b * 2 + 2)
                for h in range(2):
                    for i in range(4):
                        t = 4 * h + i
                        last = pe.matmul(bank[4 + h][:, i * D:i * D + D], qT[:, t * P:t * P + P], wout_sb[:],
                                         start=True, stop=True)
                    last.then_inc(a_out_ps, 1)
                pe.wait_ge(a_xn2, b + 1)
                transposes(lambda i: xn[:, i, :], a_xn2T_ps)

            with pe.Fori(0, DEPTH) as l:
                pe.wait_ge(attn_in, (l + 1) * NATTN * 16)

                def slot(j, t, n):
                    u = l * UNITS + t * QUADS + j + 1
                    r = j % 2
                    if on(n, 0):
                        if j == 0:
                            pe.wait_ge(xw_ready, l * TILES + t + 2)
                        pe.wait_ge(square_done, u)
                        pe.wait_ge(qrot_done, u)
                        pe.wait_ge(kn_done, u)
                        pe.matmul(bank[0][:], xw[:, WIN:KW], wqk[:, j].rearrange("p a n -> p (a n)"),
                                  start=True, stop=True).then_inc(proj_done, 1)
                        pe.wait_ge(v_kept, u)
                        for g in range(2):
                            last = pe.matmul(bank[1][0:GK, g * QC:(g + 1) * QC], xw[:, g * GQ:g * GQ + GK],
                                             wv[:, j * QC:(j + 1) * QC], start=True, stop=True)
                        last.then_inc(v_done, 1)
                    if on(n, 1):
                        pe.wait_ge(qk_kept, u - 1)
                        pe.wait_ge(qrot_done, u)
                        pe.wait_ge(krot_done, u)
                        for c in range(4):
                            for part in range(2):
                                src = rot[:, (j - 1) % 2, c // 2, part].rearrange("p h d -> p (h d)")
                                last = pe.matmul(bank[2][:, c * P:c * P + P], src[:, (c % 2) * P:(c % 2 + 1) * P],
                                                 ident[:], is_transpose=True, start=(part == 0), stop=(part == 1))
                        last.then_inc(qkT_done, 1)
                    if on(n, 2):
                        pe.wait_ge(probs_done, u - 1)
                        for h in range(QH):
                            last = pe.transpose(bank[5][0:GK, h * P:h * P + P], probs[:, h, :], ident[:])
                        last.then_inc(pT_done, 1)
                    if on(n, 1):
                        before = (j - 1) % QUADS
                        pe.wait_ge(qk_kept, u)
                        pe.wait_ge(max_done, u - 1)
                        alone(pe)
                        for h in range(QH):
                            rows = slice(64 * (h % 2), 64 * (h % 2) + 64)
                            c = h // 2
                            for g in range(2):
                                last = pe.matmul(bank[3 + h % 2][g * GQ:(g + 1) * GQ, c * GK:(c + 1) * GK],
                                                 qk[rows, before, c, WIN + g * GQ:WIN + (g + 1) * GQ],
                                                 qk[rows, before, 2 + c, g * GQ:g * GQ + GK],
                                                 start=True, stop=True)
                        last.then_inc(s_done, 1)
                    if on(n, 2):
                        two = (j - 2) % QUADS
                        pe.wait_ge(pT_kept, u - 1)
                        pe.wait_ge(v_kept, u - 1)
                        pe.wait_ge(o_kept, u - 2)
                        for h in range(QH):
                            c, side = h // 2, h % 2
                            for g in range(2):
                                last = pe.matmul(bank[6][64 * side:64 * side + 64, c * P + g * GQ:c * P + (g + 1) * GQ],
                                                 vs[:, two, g, h * DH:(h + 1) * DH],
                                                 pT[:, h * P + g * GQ:h * P + (g + 1) * GQ], start=True, stop=True)
                        last.then_inc(o_done, 1)
                    if on(n, 3):
                        three = (j - 3) % QUADS
                        pe.wait_ge(o_kept, u - 2)
                        if three == 0:
                            pe.wait_ge(y_written, l * TILES + t + 1)
                        for c in range(2):
                            last = pe.matmul(bank[7][:, 0:P], wo[:, 2 * three + c, :],
                                             oT[:, (j - 3 + 2) % 2, c * P:c * P + P],
                                             start=(three == 0 and c == 0), stop=(three == 3 and c == 1))
                        if three == 3:
                            last.then_inc(y_done, 1)

                pipeline(pe, slot)

                pe.wait_ge(ffn_in, (l + 1) * NFFN * 16)
                pe.wait_ge(y_written, (l + 1) * TILES + 1)
                alone(pe)
                with pe.Fori(0, B) as b:
                    v0 = l * 2 * B + b * 2
                    for h in range(2):
                        pe.matmul(bank[h][:], ones[:], Y[:, bass.ds(b * XB + WIN + h * FT, FT)],
                                  start=True, stop=True).then_inc(mean_done, 1)
                    for h in range(2):
                        pe.wait_ge(fsq_done, v0 + h + 1)
                        for i in range(FT // P):
                            last = pe.matmul(bank[h][:, i:i + 1], fsq[:, h, i * P:i * P + P], ones[:, 0:1],
                                             start=True, stop=True)
                        last.then_inc(var_done, 1)
                    for h in range(2):
                        pe.wait_ge(fdiag_done, v0 + h + 1)
                        pe.matmul(bank[h][:], one[:], fdiag[:, h], start=True, stop=True).then_inc(spread_done, 1)

                    def up(h, k):
                        c0, cn = HCH[k]
                        if k == 0:
                            pe.wait_ge(faff_done, v0 + h + 1)
                        if h or k == 2:
                            pe.wait_ge(hid_done, (v0 + h) * CH + k - 1)
                        pe.matmul(bank[2 + (h + k) % 2][0:cn, :], w1[:, HID + c0:HID + c0 + cn], fxn[:, h],
                                  start=True, stop=True)
                        pe.matmul(bank[4 + (h + k) % 2][0:cn, :], w1[:, c0:c0 + cn], fxn[:, h],
                                  start=True, stop=True).then_inc(up_done, 1)

                    def down(h):
                        pe.wait_ge(hid_done, (v0 + h + 1) * CH)
                        for k, (c0, cn) in enumerate(HCH):
                            last = pe.matmul(bank[6 + h][:], w2[0:cn, k, :], hidden[0:cn, h, k, :],
                                             start=(k == 0), stop=(k == CH - 1))
                        last.then_inc(down_done, 1)

                    for k in range(CH):
                        up(0, k)
                    up(1, 0)
                    up(1, 1)
                    down(0)
                    up(1, 2)
                    down(1)

            with pe.Fori(0, B) as b:
                pe.wait_ge(z_xT, b + 1)
                pe.wait_ge(z_x, b * 2 + 1)
                for i in range(TPB):
                    last = pe.transpose(bank[i // 4][:, (i % 4) * P:(i % 4 + 1) * P], ctxT[:, i * P:i * P + P], ident[:])
                last.then_inc(z_x_ps, 1)


def rotary_tables():
    half = np.arange(0, DH, 2, dtype=np.float32)
    inv_freq = (1.0 / np.float32(10000.0) ** (half / np.float32(DH))).astype(np.float32)
    t = np.arange(S, dtype=np.float32)
    freqs = (t[:, None] * inv_freq[None, :]).astype(np.float64)
    base = ((half + np.float32(0.4 * DH)) / np.float32(1.4 * DH)).astype(np.float64)
    power = ((t - S // 2) / (WIN // 2)).astype(np.float64)
    scale = base[None, :] ** power[:, None]
    tab = np.zeros((S, 2, 2, DH), np.float64)
    for side, s in enumerate((scale * 8.0, 1.0 / scale)):
        tab[:, side, 0, :HALF] = tab[:, side, 0, HALF:] = np.cos(freqs) * s
        tab[:, side, 1, :HALF] = np.sin(freqs) * s
        tab[:, side, 1, HALF:] = -np.sin(freqs) * s
    return np.ascontiguousarray(tab.reshape(TPB, P, 2, 2, DH).transpose(1, 0, 2, 3, 4)).astype(np.float32)


def band_masks():
    q = (np.arange(P) % GQ)[:, None, None]
    k = np.arange(GK)[None, None, :] - WIN
    first = (np.arange(TPB) == 0)[None, :, None] & (np.arange(P) < GQ)[:, None, None]
    seen = (k <= q) & (k >= q - WIN) & ~(first & (k < 0))
    return np.where(seen, np.float32(0), np.float32(MASKED)).astype(np.float32)


def kernel(**inputs):
    import concourse.bacc as bacc
    from concourse.bass_utils import run_bass_kernel_spmd

    a = {k: np.ascontiguousarray(v) for k, v in inputs.items()}
    w = a["L0_attn_Wqkv_w"]
    group = np.arange(P) // A_HEAD
    same = (group[:, None] == group[None, :]).astype(np.float32)
    arrays = {
        "x": a["L0_attn_x"],
        "wkv_t": np.ascontiguousarray(w[D:].T), "bkv": a["L0_attn_Wqkv_b"][D:],
        "wq_t": np.ascontiguousarray(w[:D].T), "bq": a["L0_attn_Wqkv_b"][:D],
        "gn_w": a["L0_attn_gn_w"], "gn_b": a["L0_attn_gn_b"],
        "wo_t": np.ascontiguousarray(a["L0_attn_out_w"].T), "bo": a["L0_attn_out_b"],
    }
    arrays |= {k: a["L0_ffn_" + k] for k in
               ("Wqkv", "q_scale", "k_scale", "Wo", "ln_g", "ln_b", "W1", "b1", "W2", "b2")}
    arrays |= {
        "rotary": rotary_tables(), "band": band_masks(), "ident_in": np.eye(P, dtype=np.float32),
        "keep_in": np.ascontiguousarray(np.broadcast_to(np.arange(TPB) > 0, (P, TPB)).astype(np.float32)),
        "block_in": np.ascontiguousarray(np.stack([same, same / np.float32(A_HEAD * S)], axis=1)),
    }
    nc = bacc.Bacc("TRN2", target_bir_lowering=False, num_devices=1)
    arrays = {f"in_{k}": np.ascontiguousarray(v) for k, v in arrays.items()}
    args = {k[3:]: nc.dram_tensor(k, v.shape, F32, kind="ExternalInput").ap() for k, v in arrays.items()}
    out = nc.dram_tensor("out_x", (B, S, D), F32, kind="ExternalOutput").ap()
    kernel_program(nc, out=out, **args)
    r = run_bass_kernel_spmd(nc, [arrays], core_ids=[0])
    return r.results[0]["out_x"]
```

```python
from contextlib import ExitStack

import numpy as np

import concourse.bass as bass
from concourse import mybir

F32 = mybir.dt.float32
ALU = mybir.AluOpType
ACT = mybir.ActivationFunctionType
AX = mybir.AxisListType

B, S, D = 4, 1024, 128
P = 128
TPB = S // P
TILES = B * TPB
DEPTH = 6
HEADS, DH, WIN = 16, 64, 32
INNER = HEADS * DH
HALF = DH // 2
QUADS = 4
QH = HEADS // QUADS
QC = QH * DH
UNITS = TILES * QUADS
GQ = P // 2
GK = GQ + WIN
KW = WIN + P
HID = int(D * 4 * 2 / 3)
HCH = [(c, min(128, HID - c)) for c in range(0, HID, 128)]
XB = WIN + S + WIN
FT = 512
A_HEAD = 4
EPS = 1e-5
MASKED = -1e30


def kernel_program(nc, x, wkv_t, bkv, wq_t, bq, gn_w, gn_b, wo_t, bo,
                   Wqkv, q_scale, k_scale, Wo, ln_g, ln_b, W1, b1, W2, b2,
                   rotary, band, ident_in, block_in, keep_in, out):
    with ExitStack() as ctx:
        def sb(name, shape):
            return ctx.enter_context(nc.sbuf_tensor(name, shape, F32))

        def sem(name):
            return ctx.enter_context(nc.semaphore(name))

        bank = [ctx.enter_context(nc.psum_tensor(f"bank{i}", [P, 512], F32)) for i in range(8)]

        X = sb("X", [P, B * XB])
        Y = sb("Y", [P, B * XB])
        resid = sb("resid", [P, TILES, D])
        ident = sb("ident", [P, P])
        block = sb("block", [P, 2, P])
        ones = sb("ones", [P, P])
        half_neg = sb("half_neg", [P, 2 * QH])

        wkv_sb = sb("wkv_sb", [P, 2 * D])
        wq_sb = sb("wq_sb", [P, D])
        wout_sb = sb("wout_sb", [P, D])
        bkv_sb = sb("bkv_sb", [P, 2 * D])
        bo_sb = sb("bo_sb", [P, D])
        cols = sb("cols", [P, 3])
        xn = sb("xn", [P, TPB, D])
        xc = sb("xc", [P, TPB, D])
        sq = sb("sq", [P, TPB, D])
        xnT = sb("xnT", [P, S])
        kv = sb("kv", [P, TPB, 2 * D])
        state = sb("state", [P, P])
        qT = sb("qT", [P, S])
        ctxT = sb("ctxT", [P, S])
        stat = sb("stat", [P, 5, TPB])
        csum = sb("csum", [P, 3])
        cssq = sb("cssq", [P, 3])
        gstat = sb("gstat", [P, 5])

        wqk = sb("wqk", [P, QUADS, 2, QC])
        wv = sb("wv", [P, INNER])
        wo = sb("wo", [P, INNER // P, D])
        scales = sb("scales", [P, 2, DH])
        tables = sb("tables", [P, TPB, 2, 2, DH])
        rotary_sb = sb("rotary_sb", [P, TPB, 2, 2, DH])
        w1 = sb("w1", [P, 2 * HID])
        w2 = sb("w2", [P, len(HCH), D])
        fcols = sb("fcols", [P, 3 + 2 * len(HCH)])

        xw = sb("xw", [P, KW])
        masks = sb("masks", [P, TPB, GK])
        mask = sb("mask", [P, GK])
        keep = sb("keep", [P, TPB])
        square = sb("square", [P, 2 * QH, DH])
        sumsq = sb("sumsq", [P, 2, 2, 2 * QH])
        rnorm = sb("rnorm", [P, QUADS, 2 * QH])
        rot = sb("rot", [P, 2, 2, 2 * QH, DH])
        qk = sb("qk", [P, QUADS, 4, KW])
        vs = sb("vs", [GK, QUADS, 2, QC])
        scores = sb("scores", [P, QH, GK])
        probs = sb("probs", [P, QH, GK])
        rowmax = sb("rowmax", [P, QH])
        nbias = sb("nbias", [P, QH])
        rowsum = sb("rowsum", [P, QH])
        rsum = sb("rsum", [P, QH])
        pT = sb("pT", [GK, QH * P])
        oT = sb("oT", [P, 2, 2 * P])

        fxc = sb("fxc", [P, 2, FT])
        fsq = sb("fsq", [P, 2, FT])
        fvar = sb("fvar", [P, 2, FT // P])
        frs = sb("frs", [P, 2, FT // P])
        fdiag = sb("fdiag", [P, 2, FT])
        one = sb("one", [P, P])
        fxn = sb("fxn", [P, 2, FT])
        gate = sb("gate", [P, 2, FT])
        hidden = sb("hidden", [P, 2, len(HCH), FT])

        def sems(names):
            return [sem(name) for name in names.split()]

        consts_in, x_in, consts_set, out_stored = sems("consts_in x_in consts_set out_stored")
        attn_in, ffn_in, tables_set = sems("attn_in ffn_in tables_set")
        ln_step, ln_rsqrt = sems("ln_step ln_rsqrt")
        (a_xn, a_xnT_ps, a_xnT, a_kv_ps, a_kv, a_state_ps, a_state, a_q_ps, a_q, a_ctx_ps, a_ctx) = sems(
            "a_xn a_xnT_ps a_xnT a_kv_ps a_kv a_state_ps a_state a_q_ps a_q a_ctx_ps a_ctx")
        (a_csum, a_mean_ps, a_mean, a_sq, a_ssq, a_var_ps, a_var, a_rs, a_scale, a_shift, a_gn) = sems(
            "a_csum a_mean_ps a_mean a_sq a_ssq a_var_ps a_var a_rs a_scale a_shift a_gn")
        (a_out_ps, a_out, a_ln2, a_x1, a_xn2, a_xn2T_ps, x_ready) = sems(
            "a_out_ps a_out a_ln2 a_x1 a_xn2 a_xn2T_ps x_ready")
        z_xT, z_x_ps, z_x, z_ln, z_out = sems("z_xT z_x_ps z_x z_ln z_out")
        proj_done, v_done, qkT_done, s_done, pT_done, o_done = sems("proj_done v_done qkT_done s_done pT_done o_done")
        square_done, v_kept, qk_kept, exp_done, o_kept = sems("square_done v_kept qk_kept exp_done o_kept")
        rot_done, ssq_done, floor_done = sems("rot_done ssq_done floor_done")
        max_done, nbias_done, rsum_done, pT_kept = sems("max_done nbias_done rsum_done pT_kept")
        rnorm_done, kscale_done, probs_done, tail_moved = sems("rnorm_done kscale_done probs_done tail_moved")
        xw_ready, mask_ready, y_done, y_written = sems("xw_ready mask_ready y_done y_written")
        mean_done, center_done, fsq_done, var_done, eps_done, frs_done, fn_done, faff_done = sems(
            "mean_done center_done fsq_done var_done eps_done frs_done fn_done faff_done")
        fdiag_done, spread_done = sems("fdiag_done spread_done")
        up_done, gelu_done, hid_done, down_done = sems("up_done gelu_done hid_done down_done")

        NCONST, NATTN, NFFN = 13, 6, 6 + 2 * len(HCH)
        NSET = 6

        def start_at_one(eng, names):
            for s in names:
                eng.sem_inc(s, 1)

        CH = len(HCH)
        blk = ctx.enter_context(nc.Block())

        def column(tile):
            return tile * P + (tile // TPB) * (XB - S)

        def alone(eng):
            eng.nop(nofuse=True)

        def on(n, lag):
            return n is None or 0 <= n - lag < UNITS

        def pipeline(eng, slot):
            for j in range(QUADS):
                slot(j, 0, j)
            with eng.Fori(1, TILES) as t:
                for j in range(QUADS):
                    slot(j, t, None)
            for j in range(QUADS):
                slot(j, TILES, UNITS + j)

        def tiles_of(b):
            return resid[:, bass.ds(b * TPB, TPB), :]

        def by_tile(ap):
            return ap.rearrange("p (t n) -> p t n", n=D)

        def over_d(col, n):
            return col[:, :, None].broadcast_to([P, n, D])

        @blk.sync
        def _(sp):
            def row(v, n):
                return v.rearrange("(a n) -> a n", a=1).broadcast_to([P, n])

            def col(v):
                return v.rearrange("(n a) -> n a", a=1)

            start_at_one(sp, (out_stored,))
            for b in range(B):
                sp.dma_start(tiles_of(b), x[b].rearrange("(n p) d -> p n d", p=P)).then_inc(x_in, 16)
            for dst, src in (
                (ident[:], ident_in), (block[:], block_in), (wkv_sb[:], wkv_t), (wq_sb[:], wq_t),
                (wout_sb[:], wo_t), (bkv_sb[:], row(bkv, 2 * D)), (bo_sb[:], row(bo, D)),
                (cols[:, 0:1], col(bq)), (cols[:, 1:2], col(gn_w)), (cols[:, 2:3], col(gn_b)),
                (rotary_sb[:], rotary), (masks[:], band), (keep[:], keep_in),
            ):
                sp.dma_start(dst, src).then_inc(consts_in, 16)
            with sp.Fori(0, DEPTH) as l:
                sp.wait_ge(y_written, l * TILES + 1)
                for dst, src in (
                    (wqk[:, :, 0, :], Wqkv[l, :, 0:INNER].rearrange("p (j n) -> p j n", j=QUADS)),
                    (wqk[:, :, 1, :], Wqkv[l, :, INNER:2 * INNER].rearrange("p (j n) -> p j n", j=QUADS)),
                    (wv[:], Wqkv[l, :, 2 * INNER:3 * INNER]),
                    (wo[:], Wo[l].rearrange("(c p) n -> p c n", p=P)),
                    (scales[:, 0, :], q_scale[l].rearrange("(a n) -> a n", a=1).broadcast_to([P, DH])),
                    (scales[:, 1, :], k_scale[l].rearrange("(a n) -> a n", a=1).broadcast_to([P, DH])),
                ):
                    sp.dma_start(dst, src).then_inc(attn_in, 16)
                sp.wait_ge(x_ready, (l + 1) * 2 * B + 1)
                for dst, src in (
                    (w1[:], W1[l]),
                    (w2[:, 0:CH - 1, :], W2[l, 0:(CH - 1) * P, :].rearrange("(c p) n -> p c n", p=P)),
                    (w2[0:HCH[-1][1], CH - 1, :], W2[l, (CH - 1) * P:HID, :]),
                    (fcols[:, 0:1], col(ln_g[l])), (fcols[:, 1:2], col(ln_b[l])), (fcols[:, 2:3], col(b2[l])),
                ):
                    sp.dma_start(dst, src).then_inc(ffn_in, 16)
                for side in range(2):
                    for c, (c0, cn) in enumerate(HCH):
                        k = 3 + side * CH + c
                        sp.dma_start(fcols[0:cn, k:k + 1],
                                     col(b1[l, side * HID + c0:side * HID + c0 + cn])).then_inc(ffn_in, 16)
            with sp.Fori(0, B) as b:
                sp.wait_ge(z_out, b + 1)
                sp.dma_start(out[b].rearrange("(n p) d -> p n d", p=P), xn[:]).then_inc(out_stored, 16)
            sp.wait_ge(out_stored, B * 16 + 1)

        @blk.vector
        def _(dve):
            def ln_stats(src, call):
                done = call * 6
                dve.tensor_reduce(stat[:, 0, :], src, AX.X, ALU.add).then_inc(ln_step, 1)
                dve.wait_ge(ln_step, done + 1)
                dve.tensor_scalar(stat[:, 1, :], stat[:, 0, :], -1.0 / D, None, ALU.mult).then_inc(ln_step, 1)
                dve.wait_ge(ln_step, done + 2)
                dve.tensor_tensor(xc[:], src, over_d(stat[:, 1, :], TPB), ALU.add).then_inc(ln_step, 1)
                dve.wait_ge(ln_step, done + 3)
                dve.tensor_tensor(sq[:], xc[:], xc[:], ALU.mult).then_inc(ln_step, 1)
                dve.wait_ge(ln_step, done + 4)
                dve.tensor_reduce(stat[:, 2, :], sq[:], AX.X, ALU.add).then_inc(ln_step, 1)
                dve.wait_ge(ln_step, done + 5)
                dve.tensor_scalar(stat[:, 3, :], stat[:, 2, :], 1.0 / D, EPS, ALU.mult, ALU.add).then_inc(ln_step, 1)

            def ln_scale(dst, call):
                dve.wait_ge(ln_rsqrt, call + 1)
                return dve.tensor_tensor(dst, xc[:], over_d(stat[:, 4, :], TPB), ALU.mult)

            start_at_one(dve, (rot_done, ssq_done, floor_done, max_done, nbias_done, rsum_done, v_kept,
                               y_written, z_x))
            dve.memset(ones[:], 1.0 / D).then_inc(consts_set, 1)
            dve.memset(one[:], 1.0).then_inc(consts_set, 1)
            dve.memset(half_neg[:], -0.5).then_inc(consts_set, 1)
            dve.memset(X[:], 0.0).then_inc(consts_set, 1)
            dve.memset(Y[:], 0.0).then_inc(consts_set, 1)
            dve.memset(qk[:], 0.0).then_inc(consts_set, 1)
            dve.wait_ge(consts_in, NCONST * 16)
            dve.wait_ge(x_in, B * 16)

            with dve.Fori(0, B) as b:
                ln_stats(tiles_of(b), b * 3)
                dve.wait_ge(a_xn2T_ps, b * 2 + 1)
                ln_scale(xn[:], b * 3).then_inc(a_xn, 1)
                for i in range(4):
                    dve.wait_ge(a_kv_ps, b * 4 + i + 1)
                    dve.tensor_tensor(kv[:, 2 * i:2 * i + 2, :],
                                      bank[2 + i][:].rearrange("p (t n) -> p t n", t=2),
                                      bkv_sb[:, None, :].broadcast_to([P, 2, 2 * D]), ALU.add).then_inc(a_kv, 1)
                dve.wait_ge(a_state_ps, b + 1)
                dve.tensor_tensor(state[:], bank[6][:, 0:P], block[:, 0, :], ALU.mult).then_inc(a_state, 1)
                dve.wait_ge(a_ctx, b * 2 + 2)
                dve.tensor_tensor(csum[:, 2:3], csum[:, 0:1], csum[:, 1:2], ALU.add).then_inc(a_csum, 1)
                dve.wait_ge(a_mean_ps, b + 1)
                dve.tensor_scalar(gstat[:, 0:1], bank[7][:, 0:1], -1.0, None, ALU.mult).then_inc(a_mean, 1)
                dve.wait_ge(a_sq, b * 2 + 2)
                dve.tensor_tensor(cssq[:, 2:3], cssq[:, 0:1], cssq[:, 1:2], ALU.add).then_inc(a_ssq, 1)
                dve.wait_ge(a_var_ps, b + 1)
                dve.tensor_scalar(gstat[:, 1:2], bank[7][:, 0:1], EPS, None, ALU.add).then_inc(a_var, 1)
                dve.wait_ge(a_rs, b + 1)
                dve.tensor_tensor(gstat[:, 3:4], gstat[:, 2:3], cols[:, 1:2], ALU.mult).then_inc(a_scale, 1)
                dve.wait_ge(a_scale, b + 1)
                dve.scalar_tensor_tensor(out=gstat[:, 4:5], in0=gstat[:, 3:4], scalar=gstat[:, 0:1],
                                         in1=cols[:, 2:3], op0=ALU.mult, op1=ALU.add).then_inc(a_shift, 1)
                for h in range(2):
                    dve.wait_ge(a_out_ps, b * 2 + h + 1)
                    dve.tensor_tensor(xn[:, 4 * h:4 * h + 4, :], by_tile(bank[4 + h][:]),
                                      bo_sb[:, None, :].broadcast_to([P, 4, D]), ALU.add).then_inc(a_out, 1)
                dve.wait_ge(a_out, b * 2 + 2)
                ln_stats(xn[:], b * 3 + 1)
                ln_scale(sq[:], b * 3 + 1).then_inc(a_ln2, 1)
                dve.wait_ge(a_ln2, b + 1)
                dve.tensor_tensor(tiles_of(b), tiles_of(b), sq[:], ALU.add).then_inc(a_x1, 1)
                dve.wait_ge(a_x1, b + 1)
                alone(dve)
                ln_stats(tiles_of(b), b * 3 + 2)
                ln_scale(xn[:], b * 3 + 2).then_inc(a_xn2, 1)

            with dve.Fori(0, DEPTH) as l:
                dve.wait_ge(attn_in, (l + 1) * NATTN * 16)
                for side in range(2):
                    dve.tensor_tensor(tables[:, :, side, :, :], rotary_sb[:, :, side, :, :],
                                      scales[:, side, None, None, :].broadcast_to([P, TPB, 2, DH]),
                                      ALU.mult).then_inc(tables_set, 1)
                dve.wait_ge(tables_set, l * 2 + 2)

                def slot(j, t, n):
                    u = l * UNITS + t * QUADS + j + 1
                    r = j % 2
                    if on(n, 3):
                        dve.wait_ge(exp_done, u - 2)
                        dve.reciprocal(rsum[:], rowsum[:]).then_inc(rsum_done, 1)
                    if on(n, 1):
                        dve.wait_ge(v_done, u)
                        dve.tensor_copy(vs[:, (j - 1) % QUADS].rearrange("p g c -> p (g c)"),
                                        bank[1][0:GK, :]).then_inc(v_kept, 1)
                    if on(n, 0):
                        dve.wait_ge(square_done, u + 1)
                        dve.tensor_reduce(sumsq[:, r, 0, :], square[:], AX.X, ALU.add).then_inc(ssq_done, 1)
                        dve.wait_ge(ssq_done, u + 1)
                        dve.tensor_scalar(sumsq[:, r, 1, :], sumsq[:, r, 0, :], 1e-24, None,
                                          ALU.max).then_inc(floor_done, 1)
                    if on(n, 2):
                        two = (j - 2) % QUADS
                        if two == 0:
                            dve.wait_ge(mask_ready, l * TILES + t + 2)
                        dve.wait_ge(s_done, u - 1)
                        alone(dve)
                        for h in range(QH):
                            last = dve.tensor_tensor_reduce(
                                scores[:, h, :], bank[3 + h % 2][:, (h // 2) * GK:(h // 2 + 1) * GK], mask[:],
                                1.0, -3e38, ALU.add, ALU.max, rowmax[:, h:h + 1])
                        last.then_inc(max_done, 1)
                        dve.wait_ge(max_done, u - 1)
                        dve.scalar_tensor_tensor(out=nbias[:], in0=rowmax[:], scalar=-1.0,
                                                 in1=rnorm[:, two, 0:QH], op0=ALU.mult,
                                                 op1=ALU.mult).then_inc(nbias_done, 1)
                    if on(n, 0):
                        tab = tables[:, bass.ds(t % TPB, 1), :, :, :].rearrange("p a s c d -> p (a s) c d")
                        heads = bank[0][:].rearrange("p (s h d) -> p s h d", s=2, h=QH)
                        parts = rot[:, r].rearrange("p c (s h) d -> p c s h d", s=2)
                        dve.tensor_tensor(parts[:, 0], heads,
                                          tab[:, :, 0, None, :].broadcast_to([P, 2, QH, DH]), ALU.mult)
                        for a in range(2):
                            here, there = slice(a * HALF, (a + 1) * HALF), slice((1 - a) * HALF, (2 - a) * HALF)
                            last = dve.tensor_tensor(parts[:, 1, :, :, there], heads[:, :, :, here],
                                                     tab[:, :, 1, None, here].broadcast_to([P, 2, QH, HALF]),
                                                     ALU.mult)
                        last.then_inc(rot_done, 1)
                    if on(n, 4) and j == 3:
                        c = column(t - 1) + WIN
                        dve.wait_ge(y_done, l * TILES + t + 1)
                        dve.tensor_tensor(Y[0:64, bass.ds(c, P)], bank[7][0:64, 0:P],
                                          X[0:64, bass.ds(c, P)], ALU.add)
                        dve.tensor_tensor(Y[64:128, bass.ds(c + 1, P)], bank[7][64:128, 0:P],
                                          X[64:128, bass.ds(c + 1, P)], ALU.add).then_inc(y_written, 1)

                pipeline(dve, slot)

                dve.wait_ge(ffn_in, (l + 1) * NFFN * 16)
                dve.wait_ge(y_written, (l + 1) * TILES + 1)
                alone(dve)
                with dve.Fori(0, B) as b:
                    v0 = l * 2 * B + b * 2
                    for h in range(2):
                        dve.wait_ge(mean_done, v0 + h + 1)
                        dve.tensor_tensor(fxc[:, h], Y[:, bass.ds(b * XB + WIN + h * FT, FT)], bank[h][:],
                                          ALU.subtract).then_inc(center_done, 1)
                    for h in range(2):
                        dve.wait_ge(var_done, v0 + h + 1)
                        dve.tensor_scalar(fvar[:, h], bank[h][:, 0:FT // P], EPS, None, ALU.add).then_inc(eps_done, 1)
                    for h in range(2):
                        dve.wait_ge(frs_done, v0 + h + 1)
                        dve.tensor_tensor(by_tile(fdiag[:, h]), ident[:, None, :].broadcast_to([P, FT // P, P]),
                                          over_d(frs[:, h], FT // P), ALU.mult).then_inc(fdiag_done, 1)
                    for h in range(2):
                        dve.wait_ge(spread_done, v0 + h + 1)
                        dve.tensor_tensor(fsq[:, h], fxc[:, h], bank[h][:], ALU.mult).then_inc(fn_done, 1)
                    for h in range(2):
                        c = b * XB + WIN + h * FT
                        for k, (c0, cn) in enumerate(HCH):
                            dve.wait_ge(gelu_done, (v0 + h) * CH + k + 1)
                            dve.scalar_tensor_tensor(out=hidden[0:cn, h, k, :], in0=bank[4 + (h + k) % 2][0:cn, :],
                                                     scalar=fcols[0:cn, 3 + k:4 + k],
                                                     in1=gate[0:cn, (h + k) % 2, :],
                                                     op0=ALU.add, op1=ALU.mult).then_inc(hid_done, 1)
                        dve.wait_ge(down_done, v0 + h + 1)
                        for side in range(2):
                            rows = slice(64 * side, 64 * side + 64)
                            last = dve.scalar_tensor_tensor(
                                out=X[rows, bass.ds(c + side, FT)], in0=bank[6 + h][rows, :],
                                scalar=fcols[rows, 2:3], in1=Y[rows, bass.ds(c + side, FT)],
                                op0=ALU.add, op1=ALU.add)
                        last.then_inc(x_ready, 1)

            with dve.Fori(0, B) as b:
                dve.wait_ge(out_stored, b * 16 + 1)
                dve.wait_ge(z_x_ps, b + 2)
                for h in range(2):
                    dve.tensor_copy(xn[:, 4 * h:4 * h + 4, :], by_tile(bank[h][:])).then_inc(z_x, 1)
                dve.wait_ge(z_x, b * 2 + 3)
                ln_stats(xn[:], b + 3 * B)
                ln_scale(sq[:], b + 3 * B).then_inc(z_ln, 1)
                dve.wait_ge(z_ln, b + 1)
                dve.tensor_tensor(xn[:], sq[:], tiles_of(b), ALU.add).then_inc(z_out, 1)

        @blk.gpsimd
        def _(pool):
            def ln_pow(call):
                pool.wait_ge(ln_step, call * 6 + 6)
                pool.tensor_tensor(stat[:, 4, :], stat[:, 3, :], half_neg[:, 0:TPB], ALU.pow).then_inc(ln_rsqrt, 1)

            start_at_one(pool, (rnorm_done, kscale_done, probs_done, tail_moved, xw_ready, mask_ready))
            pool.wait_ge(consts_set, NSET)
            with pool.Fori(0, B) as b:
                ln_pow(b * 3)
                pool.wait_ge(a_var, b + 1)
                pool.tensor_tensor(gstat[:, 2:3], gstat[:, 1:2], half_neg[:, 0:1], ALU.pow).then_inc(a_rs, 1)
                ln_pow(b * 3 + 1)
                ln_pow(b * 3 + 2)

            with pool.Fori(0, DEPTH) as l:
                pool.wait_ge(x_ready, (l + 1) * 2 * B + 1)
                pool.wait_ge(tables_set, l * 2 + 2)

                def slot(j, t, n):
                    u = l * UNITS + t * QUADS + j + 1
                    r = j % 2
                    if on(n, 0) and j == 0:
                        pool.wait_ge(v_done, u)
                        alone(pool)
                        pool.tensor_copy(xw[:], X[:, bass.ds(column(t), KW)]).then_inc(xw_ready, 1)
                    if on(n, 2) and j == 2:
                        pool.wait_ge(max_done, u - 2)
                        alone(pool)
                        pool.tensor_copy(mask[:], masks[:, bass.ds(t % TPB, 1), :].rearrange(
                            "p a k -> p (a k)")).then_inc(mask_ready, 1)
                    if on(n, 1):
                        pool.wait_ge(rnorm_done, u)
                        pool.wait_ge(rot_done, u)
                        k_heads = rot[:, 1 - r, :, QH:2 * QH, :]
                        pool.tensor_tensor(k_heads, k_heads,
                                           rnorm[:, (j - 1) % QUADS, None, QH:2 * QH, None].broadcast_to([P, 2, QH, DH]),
                                           ALU.mult).then_inc(kscale_done, 1)
                    if on(n, 3):
                        pool.wait_ge(rsum_done, u - 2)
                        pool.tensor_tensor(probs[:], probs[:], rsum[:, :, None].broadcast_to([P, QH, GK]),
                                           ALU.mult).then_inc(probs_done, 1)
                    if on(n, 0):
                        if n is None:
                            pool.wait_ge(s_done, u - 3)
                            alone(pool)
                        pool.tensor_tensor(qk[:, j, 2:4, 0:WIN], qk[:, j, 2:4, P:KW],
                                           keep[:, bass.ds(t % TPB, 1), None].broadcast_to([P, 2, WIN]),
                                           ALU.mult).then_inc(tail_moved, 1)
                    if on(n, 0):
                        pool.wait_ge(floor_done, u + 1)
                        pool.tensor_tensor(rnorm[:, j, :], sumsq[:, r, 1, :], half_neg[:, 0:2 * QH],
                                           ALU.pow).then_inc(rnorm_done, 1)

                pipeline(pool, slot)

                with pool.Fori(0, B) as b:
                    for h in range(2):
                        pool.wait_ge(eps_done, l * 2 * B + b * 2 + h + 1)
                        pool.tensor_tensor(frs[:, h], fvar[:, h], half_neg[:, 0:FT // P], ALU.pow).then_inc(frs_done, 1)

            with pool.Fori(0, B) as b:
                ln_pow(b + 3 * B)

        @blk.scalar
        def _(act):
            start_at_one(act, (square_done, pT_kept, qk_kept, exp_done, o_kept, x_ready))
            act.wait_ge(consts_in, NCONST * 16)
            act.wait_ge(consts_set, NSET)
            with act.Fori(0, B) as b:
                for h in range(2):
                    act.wait_ge(a_xnT_ps, b * 2 + h + 1)
                    act.activation(xnT[:, 512 * h:512 * h + 512], bank[h][:], ACT.Copy).then_inc(a_xnT, 1)
                act.wait_ge(a_q_ps, b + 1)
                for h in range(2):
                    act.activation(qT[:, 512 * h:512 * h + 512], bank[h][:], ACT.Identity,
                                   bias=cols[:, 0:1]).then_inc(a_q, 1)
                act.wait_ge(a_ctx_ps, b + 1)
                for h in range(2):
                    act.activation(ctxT[:, 512 * h:512 * h + 512], bank[2 + h][:], ACT.Copy,
                                   accum_out=csum[:, h:h + 1]).then_inc(a_ctx, 1)
                act.wait_ge(a_mean, b + 1)
                act.wait_ge(a_ctx, b * 2 + 2)
                for h in range(2):
                    act.activation(xnT[:, 512 * h:512 * h + 512], ctxT[:, 512 * h:512 * h + 512], ACT.Square,
                                   bias=gstat[:, 0:1], accum_out=cssq[:, h:h + 1]).then_inc(a_sq, 1)
                act.wait_ge(a_shift, b + 1)
                for h in range(2):
                    act.activation(qT[:, 512 * h:512 * h + 512], ctxT[:, 512 * h:512 * h + 512], ACT.Identity,
                                   scale=gstat[:, 3:4], bias=gstat[:, 4:5]).then_inc(a_gn, 1)
                for h in range(2):
                    act.wait_ge(a_xn2T_ps, b * 2 + h + 2)
                    for side in range(2):
                        rows = slice(64 * side, 64 * side + 64)
                        last = act.activation(X[rows, bass.ds(b * XB + WIN + h * 512 + side, 512)],
                                              bank[h][rows, :], ACT.Copy)
                    last.then_inc(x_ready, 1)

            with act.Fori(0, DEPTH) as l:
                def slot(j, t, n):
                    u = l * UNITS + t * QUADS + j + 1
                    if on(n, 2):
                        act.wait_ge(tail_moved, u - 1)
                        act.wait_ge(qkT_done, u - 1)
                        act.activation(qk[:, (j - 2) % QUADS, :, WIN:KW], bank[2][:].rearrange("p (c k) -> p c k", c=4),
                                       ACT.Copy).then_inc(qk_kept, 1)
                    if on(n, 0):
                        act.wait_ge(ssq_done, u)
                        act.wait_ge(proj_done, u + 1)
                        act.activation(square[:].rearrange("p h d -> p (h d)"), bank[0][:],
                                       ACT.Square).then_inc(square_done, 1)
                    if on(n, 3):
                        act.wait_ge(pT_done, u - 2)
                        act.activation(pT[:], bank[5][0:GK, :], ACT.Copy).then_inc(pT_kept, 1)
                    if on(n, 2):
                        two = (j - 2) % QUADS
                        act.wait_ge(nbias_done, u - 1)
                        for h in range(QH):
                            last = act.activation(probs[:, h, :], scores[:, h, :], ACT.Exp, bias=nbias[:, h:h + 1],
                                                  scale=rnorm[:, two, h:h + 1], accum_out=rowsum[:, h:h + 1])
                        last.then_inc(exp_done, 1)
                    if on(n, 3):
                        act.wait_ge(o_done, u - 2)
                        act.activation(oT[:, (j - 3) % 2, :], bank[6][:, 0:2 * P], ACT.Copy).then_inc(o_kept, 1)

                pipeline(act, slot)

                act.wait_ge(ffn_in, (l + 1) * NFFN * 16)
                with act.Fori(0, B) as b:
                    v0 = l * 2 * B + b * 2
                    for h in range(2):
                        act.wait_ge(center_done, v0 + h + 1)
                        act.activation(fsq[:, h], fxc[:, h], ACT.Square).then_inc(fsq_done, 1)
                    for h in range(2):
                        act.wait_ge(fn_done, v0 + h + 1)
                        act.activation(fxn[:, h], fsq[:, h], ACT.Identity, scale=fcols[:, 0:1],
                                       bias=fcols[:, 1:2]).then_inc(faff_done, 1)
                    for h in range(2):
                        for k, (c0, cn) in enumerate(HCH):
                            act.wait_ge(up_done, (v0 + h) * CH + k + 1)
                            act.activation(gate[0:cn, (h + k) % 2, :], bank[2 + (h + k) % 2][0:cn, :], ACT.Gelu,
                                           bias=fcols[0:cn, 3 + CH + k:4 + CH + k]).then_inc(gelu_done, 1)

            with act.Fori(0, B) as b:
                act.wait_ge(x_ready, (DEPTH + 1) * 2 * B + 1)
                act.wait_ge(z_x_ps, b + 1)
                for side in range(2):
                    rows = slice(64 * side, 64 * side + 64)
                    last = act.activation(ctxT[rows, :], X[rows, bass.ds(b * XB + WIN + side, S)], ACT.Copy)
                last.then_inc(z_xT, 1)

        @blk.tensor
        def _(pe):
            start_at_one(pe, (proj_done, v_done, qkT_done, s_done, pT_done, o_done, y_done, a_xn2T_ps, z_x_ps))
            pe.wait_ge(consts_in, NCONST * 16)
            pe.wait_ge(consts_set, NSET)

            def transposes(src, done):
                for h in range(2):
                    for i in range(4):
                        last = pe.transpose(bank[h][:, i * P:i * P + P], src(4 * h + i), ident[:])
                    last.then_inc(done, 1)

            with pe.Fori(0, B) as b:
                pe.wait_ge(x_ready, b * 2 + 1)
                pe.wait_ge(a_xn, b + 1)
                transposes(lambda i: xn[:, i, :], a_xnT_ps)
                for i in range(TPB):
                    if i % 4 == 0:
                        pe.wait_ge(a_xnT, b * 2 + i // 4 + 1)
                    last = pe.matmul(bank[2 + i // 2][:, (i % 2) * 2 * D:(i % 2 + 1) * 2 * D],
                                     xnT[:, i * P:i * P + P], wkv_sb[:], start=True, stop=True)
                    if i % 2:
                        last.then_inc(a_kv_ps, 1)
                for h in range(2):
                    last = pe.matmul(bank[h][:], wq_sb[:], xnT[:, 512 * h:512 * h + 512], start=True, stop=True)
                last.then_inc(a_q_ps, 1)
                for i in range(TPB):
                    if i % 2 == 0:
                        pe.wait_ge(a_kv, b * 4 + i // 2 + 1)
                    last = pe.matmul(bank[6][:, 0:P], kv[:, i, 0:D], kv[:, i, D:2 * D],
                                     start=(i == 0), stop=(i == TPB - 1))
                last.then_inc(a_state_ps, 1)
                pe.wait_ge(a_q, b * 2 + 2)
                pe.wait_ge(a_state, b + 1)
                for h in range(2):
                    last = pe.matmul(bank[2 + h][:], state[:], qT[:, 512 * h:512 * h + 512], start=True, stop=True)
                last.then_inc(a_ctx_ps, 1)
                pe.wait_ge(a_csum, b + 1)
                pe.matmul(bank[7][:, 0:1], block[:, 1, :], csum[:, 2:3], start=True, stop=True).then_inc(a_mean_ps, 1)
                pe.wait_ge(a_mean, b + 1)
                pe.wait_ge(a_ssq, b + 1)
                pe.matmul(bank[7][:, 0:1], block[:, 1, :], cssq[:, 2:3], start=True, stop=True).then_inc(a_var_ps, 1)
                pe.wait_ge(a_gn, b * 2 + 2)
                for h in range(2):
                    for i in range(4):
                        t = 4 * h + i
                        last = pe.matmul(bank[4 + h][:, i * D:i * D + D], qT[:, t * P:t * P + P], wout_sb[:],
                                         start=True, stop=True)
                    last.then_inc(a_out_ps, 1)
                pe.wait_ge(a_xn2, b + 1)
                transposes(lambda i: xn[:, i, :], a_xn2T_ps)

            with pe.Fori(0, DEPTH) as l:
                pe.wait_ge(attn_in, (l + 1) * NATTN * 16)

                def slot(j, t, n):
                    u = l * UNITS + t * QUADS + j + 1
                    if on(n, 2):
                        pe.wait_ge(qk_kept, u - 2)
                        pe.wait_ge(kscale_done, u - 1)
                        for c in range(4):
                            for part in range(2):
                                src = rot[:, j % 2, part, 2 * c:2 * c + 2].rearrange("p h d -> p (h d)")
                                last = pe.matmul(bank[2][:, c * P:c * P + P], src, ident[:], is_transpose=True,
                                                 start=(part == 0), stop=(part == 1))
                        last.then_inc(qkT_done, 1)
                    if on(n, 0):
                        if j == 0:
                            pe.wait_ge(xw_ready, l * TILES + t + 2)
                        pe.wait_ge(square_done, u)
                        pe.wait_ge(rot_done, u)
                        pe.matmul(bank[0][:], xw[:, WIN:KW], wqk[:, j].rearrange("p a n -> p (a n)"),
                                  start=True, stop=True).then_inc(proj_done, 1)
                    if on(n, 4):
                        pe.wait_ge(o_kept, u - 3)
                        if j == 0:
                            pe.wait_ge(y_written, l * TILES + t)
                        for c in range(2):
                            last = pe.matmul(bank[7][:, 0:P], wo[:, 2 * j + c, :], oT[:, j % 2, c * P:c * P + P],
                                             start=(j == 0 and c == 0), stop=(j == 3 and c == 1))
                        if j == 3:
                            last.then_inc(y_done, 1)
                    if on(n, 2):
                        two = (j - 2) % QUADS
                        pe.wait_ge(qk_kept, u - 1)
                        pe.wait_ge(max_done, u - 2)
                        alone(pe)
                        for h in range(QH):
                            rows = slice(64 * (h % 2), 64 * (h % 2) + 64)
                            c = h // 2
                            for g in range(2):
                                last = pe.matmul(bank[3 + h % 2][g * GQ:(g + 1) * GQ, c * GK:(c + 1) * GK],
                                                 qk[rows, two, c, WIN + g * GQ:WIN + (g + 1) * GQ],
                                                 qk[rows, two, 2 + c, g * GQ:g * GQ + GK],
                                                 start=True, stop=True)
                        last.then_inc(s_done, 1)
                    if on(n, 3):
                        pe.wait_ge(probs_done, u - 2)
                        for h in range(QH):
                            last = pe.transpose(bank[5][0:GK, h * P:h * P + P], probs[:, h, :], ident[:])
                        last.then_inc(pT_done, 1)
                    if on(n, 0):
                        pe.wait_ge(v_kept, u)
                        for g in range(2):
                            last = pe.matmul(bank[1][0:GK, g * QC:(g + 1) * QC], xw[:, g * GQ:g * GQ + GK],
                                             wv[:, j * QC:(j + 1) * QC], start=True, stop=True)
                        last.then_inc(v_done, 1)
                    if on(n, 3):
                        three = (j - 3) % QUADS
                        pe.wait_ge(pT_kept, u - 2)
                        pe.wait_ge(v_kept, u - 2)
                        for h in range(QH):
                            c, side = h // 2, h % 2
                            for g in range(2):
                                last = pe.matmul(bank[6][64 * side:64 * side + 64, c * P + g * GQ:c * P + (g + 1) * GQ],
                                                 vs[:, three, g, h * DH:(h + 1) * DH],
                                                 pT[:, h * P + g * GQ:h * P + (g + 1) * GQ], start=True, stop=True)
                        last.then_inc(o_done, 1)

                pipeline(pe, slot)

                pe.wait_ge(ffn_in, (l + 1) * NFFN * 16)
                pe.wait_ge(y_written, (l + 1) * TILES + 1)
                alone(pe)
                with pe.Fori(0, B) as b:
                    v0 = l * 2 * B + b * 2
                    for h in range(2):
                        pe.matmul(bank[h][:], ones[:], Y[:, bass.ds(b * XB + WIN + h * FT, FT)],
                                  start=True, stop=True).then_inc(mean_done, 1)
                    for h in range(2):
                        pe.wait_ge(fsq_done, v0 + h + 1)
                        for i in range(FT // P):
                            last = pe.matmul(bank[h][:, i:i + 1], fsq[:, h, i * P:i * P + P], ones[:, 0:1],
                                             start=True, stop=True)
                        last.then_inc(var_done, 1)
                    for h in range(2):
                        pe.wait_ge(fdiag_done, v0 + h + 1)
                        pe.matmul(bank[h][:], one[:], fdiag[:, h], start=True, stop=True).then_inc(spread_done, 1)

                    def up(h, k):
                        c0, cn = HCH[k]
                        if k == 0:
                            pe.wait_ge(faff_done, v0 + h + 1)
                        if h or k == 2:
                            pe.wait_ge(hid_done, (v0 + h) * CH + k - 1)
                        pe.matmul(bank[2 + (h + k) % 2][0:cn, :], w1[:, HID + c0:HID + c0 + cn], fxn[:, h],
                                  start=True, stop=True)
                        pe.matmul(bank[4 + (h + k) % 2][0:cn, :], w1[:, c0:c0 + cn], fxn[:, h],
                                  start=True, stop=True).then_inc(up_done, 1)

                    def down(h):
                        pe.wait_ge(hid_done, (v0 + h + 1) * CH)
                        for k, (c0, cn) in enumerate(HCH):
                            last = pe.matmul(bank[6 + h][:], w2[0:cn, k, :], hidden[0:cn, h, k, :],
                                             start=(k == 0), stop=(k == CH - 1))
                        last.then_inc(down_done, 1)

                    for k in range(CH):
                        up(0, k)
                    up(1, 0)
                    up(1, 1)
                    down(0)
                    up(1, 2)
                    down(1)

            with pe.Fori(0, B) as b:
                pe.wait_ge(z_xT, b + 1)
                pe.wait_ge(z_x, b * 2 + 1)
                for i in range(TPB):
                    last = pe.transpose(bank[i // 4][:, (i % 4) * P:(i % 4 + 1) * P], ctxT[:, i * P:i * P + P], ident[:])
                last.then_inc(z_x_ps, 1)


def rotary_tables():
    half = np.arange(0, DH, 2, dtype=np.float32)
    inv_freq = (1.0 / np.float32(10000.0) ** (half / np.float32(DH))).astype(np.float32)
    t = np.arange(S, dtype=np.float32)
    freqs = (t[:, None] * inv_freq[None, :]).astype(np.float64)
    base = ((half + np.float32(0.4 * DH)) / np.float32(1.4 * DH)).astype(np.float64)
    power = ((t - S // 2) / (WIN // 2)).astype(np.float64)
    scale = base[None, :] ** power[:, None]
    tab = np.zeros((S, 2, 2, DH), np.float64)
    for side, s in enumerate((scale * 8.0, 1.0 / scale)):
        tab[:, side, 0, :HALF] = tab[:, side, 0, HALF:] = np.cos(freqs) * s
        tab[:, side, 1, :HALF] = np.sin(freqs) * s
        tab[:, side, 1, HALF:] = -np.sin(freqs) * s
    return np.ascontiguousarray(tab.reshape(TPB, P, 2, 2, DH).transpose(1, 0, 2, 3, 4)).astype(np.float32)


def band_masks():
    q = (np.arange(P) % GQ)[:, None, None]
    k = np.arange(GK)[None, None, :] - WIN
    first = (np.arange(TPB) == 0)[None, :, None] & (np.arange(P) < GQ)[:, None, None]
    seen = (k <= q) & (k >= q - WIN) & ~(first & (k < 0))
    return np.where(seen, np.float32(0), np.float32(MASKED)).astype(np.float32)


def kernel(**inputs):
    import concourse.bacc as bacc
    from concourse.bass_utils import run_bass_kernel_spmd

    a = {k: np.ascontiguousarray(v) for k, v in inputs.items()}
    w = a["L0_attn_Wqkv_w"]
    group = np.arange(P) // A_HEAD
    same = (group[:, None] == group[None, :]).astype(np.float32)
    arrays = {
        "x": a["L0_attn_x"],
        "wkv_t": np.ascontiguousarray(w[D:].T), "bkv": a["L0_attn_Wqkv_b"][D:],
        "wq_t": np.ascontiguousarray(w[:D].T), "bq": a["L0_attn_Wqkv_b"][:D],
        "gn_w": a["L0_attn_gn_w"], "gn_b": a["L0_attn_gn_b"],
        "wo_t": np.ascontiguousarray(a["L0_attn_out_w"].T), "bo": a["L0_attn_out_b"],
    }
    arrays |= {k: a["L0_ffn_" + k] for k in
               ("Wqkv", "q_scale", "k_scale", "Wo", "ln_g", "ln_b", "W1", "b1", "W2", "b2")}
    arrays |= {
        "rotary": rotary_tables(), "band": band_masks(), "ident_in": np.eye(P, dtype=np.float32),
        "keep_in": np.ascontiguousarray(np.broadcast_to(np.arange(TPB) > 0, (P, TPB)).astype(np.float32)),
        "block_in": np.ascontiguousarray(np.stack([same, same / np.float32(A_HEAD * S)], axis=1)),
    }
    nc = bacc.Bacc("TRN2", target_bir_lowering=False, num_devices=1)
    arrays = {f"in_{k}": np.ascontiguousarray(v) for k, v in arrays.items()}
    args = {k[3:]: nc.dram_tensor(k, v.shape, F32, kind="ExternalInput").ap() for k, v in arrays.items()}
    out = nc.dram_tensor("out_x", (B, S, D), F32, kind="ExternalOutput").ap()
    kernel_program(nc, out=out, **args)
    r = run_bass_kernel_spmd(nc, [arrays], core_ids=[0])
    return r.results[0]["out_x"]
```

```python
from contextlib import ExitStack

import numpy as np

import concourse.bass as bass
from concourse import mybir

F32 = mybir.dt.float32
F32R = mybir.dt.float32r
ALU = mybir.AluOpType
ACT = mybir.ActivationFunctionType
AX = mybir.AxisListType

B, S, D = 4, 1024, 128
P = 128
TPB = S // P
TILES = B * TPB
DEPTH = 6
HEADS, DH, WIN = 16, 64, 32
INNER = HEADS * DH
HALF = DH // 2
QUADS = 4
QH = HEADS // QUADS
QC = QH * DH
UNITS = TILES * QUADS
WINDOW_SLOT = 3
LAGS = 6
GQ = P // 2
GK = GQ + WIN
KW = WIN + P
HID = int(D * 4 * 2 / 3)
HCH = [(c, min(128, HID - c)) for c in range(0, HID, 128)]
XB = WIN + S + WIN
FT = 512
A_HEAD = 4
EPS = 1e-5
assert B == QUADS
MASKED = -1e30


def kernel_program(nc, x, wkv_t, bkv, wq_t, bq, gn_w, gn_b, wo_t, bo,
                   Wqkv, q_scale, k_scale, Wo, ln_g, ln_b, W1, b1, W2, b2,
                   rotary, band, ident_in, block_in, keep_in, out):
    with ExitStack() as ctx:
        def sb(name, shape, dtype=F32):
            return ctx.enter_context(nc.sbuf_tensor(name, shape, dtype))

        def sem(name):
            return ctx.enter_context(nc.semaphore(name))

        bank = [ctx.enter_context(nc.psum_tensor(f"bank{i}", [P, 512], F32)) for i in range(8)]

        X = sb("X", [P, B * XB + KW])
        Y = sb("Y", [P, B * XB])
        resid = sb("resid", [P, TILES, D])
        ident = sb("ident", [P, P])
        block = sb("block", [P, 2, P])
        half_neg = sb("half_neg", [P, 2 * QH])

        wkv_sb = sb("wkv_sb", [P, 2 * D])
        wq_sb = sb("wq_sb", [P, D])
        wout_sb = sb("wout_sb", [P, D])
        bkv_sb = sb("bkv_sb", [P, 2 * D])
        bo_sb = sb("bo_sb", [P, D])
        cols = sb("cols", [P, 3])
        norms = sb("norms", [P, 3 * S])
        ffn_work = sb("ffn_work", [P, 6 * FT])
        xn, xn_b, scaled = (norms[:, i * S:(i + 1) * S].rearrange("p (t n) -> p t n", t=TPB) for i in range(3))
        early = sb("early", [P, 4 * S])
        xnT = early[:, 0:S]
        qT = early[:, S:2 * S]
        kv = early[:, 2 * S:4 * S].rearrange("p (t n) -> p t n", t=TPB)
        state = sb("state", [P, P])
        ctxT = sb("ctxT", [P, S])
        ln_parts = sb("ln_parts", [P, 2, TPB, 6])
        ln_mv = sb("ln_mv", [P, 2, TPB, 2])
        ln_var = sb("ln_var", [P, 2, TPB])
        ln_rs = sb("ln_rs", [P, 2, TPB])
        csum = sb("csum", [P, 3])
        cssq = sb("cssq", [P, 3])
        gstat = sb("gstat", [P, 5])

        wqkv, wqkv_first = (buffer[:, 0:3 * INNER].rearrange("p (j s n) -> p j s n", j=QUADS, s=3)
                            for buffer in (norms, ffn_work))
        wqkv_hi = sb("wqkv_hi", [P, QUADS, 3, QC], F32R)
        wqkv_lo = sb("wqkv_lo", [P, QUADS, 3, QC], F32R)
        wo = sb("wo", [P, INNER // P, D])
        scales = sb("scales", [P, 2, DH])
        tables = sb("tables", [P, TPB, 2, 2, DH])
        rotary_sb = sb("rotary_sb", [P, TPB, 2, 2, DH])
        w1 = sb("w1", [P, 2 * HID])
        w1_hi = sb("w1_hi", [P, 2 * HID], F32R)
        w1_lo = sb("w1_lo", [P, 2 * HID], F32R)
        w2 = sb("w2", [P, len(HCH), D])
        fcols = sb("fcols", [P, 3 + 2 * len(HCH)])

        xw = sb("xw", [P, 2, 2, KW], F32R)
        masks = sb("masks", [P, TPB, GK])
        mask = sb("mask", [P, GK])
        keep = sb("keep", [P, TPB])
        square = sb("square", [P, 2 * QH, DH])
        sumsq = sb("sumsq", [P, 2, 2, 2 * QH])
        rnorm = sb("rnorm", [P, QUADS, 2 * QH])
        rot = sb("rot", [P, 2, 2, 2 * QH, DH])
        qk = sb("qk", [P, QUADS, 4, KW])
        vs = sb("vs", [GK, QUADS, 2, QC])
        scores = sb("scores", [P, 2, QH, GK])
        probs = sb("probs", [P, QH, GK])
        rowmax = sb("rowmax", [P, QH])
        nbias = sb("nbias", [P, 2, QH])
        rowsum = sb("rowsum", [P, QH])
        rsum = sb("rsum", [P, QH])
        pT = sb("pT", [GK, QH * P])
        oT = sb("oT", [P, 2, 2 * P])

        y_part = ctxT[:].rearrange("p (h n) -> p h n", h=2)
        FTT = FT // P
        fstat = sb("fstat", [P, 2, FTT, 6])
        fmv = sb("fmv", [P, 2, FTT, 2])
        fvar = sb("fvar", [P, 2, FTT])
        frs = sb("frs", [P, 2, FTT])
        fnorm = ffn_work[:, 0:2 * FT].rearrange("p (h i n) -> p h i n", h=2, i=FTT)
        fxn = ffn_work[:, 2 * FT:4 * FT].rearrange("p (h n) -> p h n", h=2)
        fxn_hi = sb("fxn_hi", [P, 2, FT], F32R)
        fxn_lo = sb("fxn_lo", [P, 2, FT], F32R)
        gate = ffn_work[:, 4 * FT:6 * FT].rearrange("p (h n) -> p h n", h=2)
        hidden = early[:, 0:2 * len(HCH) * FT].rearrange("p (h k n) -> p h k n", h=2, k=len(HCH))

        def sems(names):
            return [sem(name) for name in names.split()]

        consts_in, x_in, consts_set, out_stored = sems("consts_in x_in consts_set out_stored")
        attn_in, ffn_in, tables_set = sems("attn_in ffn_in tables_set")
        w_high, w_split, xw_high, w1_high, w1_split = sems("w_high w_split xw_high w1_high w1_split")
        ln_parts_done, ln_mv_done, ln_var_done, ln_rs_done = (
            sems(f"{name}_0 {name}_1") for name in ("ln_parts_done", "ln_mv_done", "ln_var_done", "ln_rs_done"))
        (a_xn, a_xnT_ps, a_xnT, a_kv_ps, a_kv, a_state_ps, a_state, a_q_ps, a_q, a_ctx_ps, a_ctx) = sems(
            "a_xn a_xnT_ps a_xnT a_kv_ps a_kv a_state_ps a_state a_q_ps a_q a_ctx_ps a_ctx")
        (a_csum, a_mean_ps, a_mean, a_sq, a_ssq, a_var_ps, a_var, a_rs, a_scale, a_shift, a_gn) = sems(
            "a_csum a_mean_ps a_mean a_sq a_ssq a_var_ps a_var a_rs a_scale a_shift a_gn")
        (a_out_ps, a_out, a_ln2, a_x1, a_xn2, a_xn2T_ps, x_ready) = sems(
            "a_out_ps a_out a_ln2 a_x1 a_xn2 a_xn2T_ps x_ready")
        z_xT, z_x_ps, z_ln, z_out = sems("z_xT z_x_ps z_ln z_out")
        proj_done, v_done, qkT_done, s_done, pT_done, o_done = sems("proj_done v_done qkT_done s_done pT_done o_done")
        square_done, v_kept, qk_kept, exp_done, o_kept = sems("square_done v_kept qk_kept exp_done o_kept")
        rot_done, qsum_done, ssq_done, floor_done = sems("rot_done qsum_done ssq_done floor_done")
        max_done, nbias_done, rsum_done, pT_kept = sems("max_done nbias_done rsum_done pT_kept")
        rnorm_done, ksum_done, kscale_done, probs_done, tail_moved = sems("rnorm_done ksum_done kscale_done probs_done tail_moved")
        xw_ready, mask_ready, y_done, y_written = sems("xw_ready mask_ready y_done y_written")
        y_copied, ft_done, fstat_done, faggr_done, eps_done, frs_done, fnorm_done = sems(
            "y_copied ft_done fstat_done faggr_done eps_done frs_done fnorm_done")
        fback_done, faff_done, fsplit_done = sems("fback_done faff_done fsplit_done")
        up_done, gelu_done, hid_done, down_done = sems("up_done gelu_done hid_done down_done")

        NCONST, NATTN, NFFN = 13, 6, 6 + 2 * len(HCH)
        NSET = 4

        def start_at_one(eng, names):
            for s in names:
                eng.sem_inc(s, 1)

        CH = len(HCH)
        blk = ctx.enter_context(nc.Block())

        def column(tile):
            return tile * P + (tile // TPB) * (XB - S)

        def alone(eng):
            eng.nop(nofuse=True)

        def on(n, lag):
            return n is None or 0 <= n - lag < UNITS

        def pipeline(eng, slot, after=lambda k: None):
            def peeled(start, stop):
                for n in range(start, stop):
                    slot(n % QUADS, n // QUADS, n, n // QUADS % 2)
                    if n >= UNITS:
                        after(n - UNITS)

            peeled(0, 2 * QUADS)
            with eng.Fori(1, TILES // 2) as pair:
                for side in range(2):
                    for j in range(QUADS):
                        slot(j, pair * 2 + side, None, side)
            peeled(UNITS, UNITS + LAGS)

        def tiles_of(b):
            return resid[:, bass.ds(b * TPB, TPB), :]

        def by_tile(ap):
            return ap.rearrange("p (t n) -> p t n", n=D)

        @blk.sync
        def _(sp):
            def row(v, n):
                return v.rearrange("(a n) -> a n", a=1).broadcast_to([P, n])

            def col(v):
                return v.rearrange("(n a) -> n a", a=1)

            start_at_one(sp, (out_stored,))
            for b in range(B):
                sp.dma_start(tiles_of(b), x[b].rearrange("(n p) d -> p n d", p=P)).then_inc(x_in, 16)
            for dst, src in (
                (ident[:], ident_in), (block[:], block_in), (wkv_sb[:], wkv_t), (wq_sb[:], wq_t),
                (wout_sb[:], wo_t), (bkv_sb[:], row(bkv, 2 * D)), (bo_sb[:], row(bo, D)),
                (cols[:, 0:1], col(bq)), (cols[:, 1:2], col(gn_w)), (cols[:, 2:3], col(gn_b)),
                (rotary_sb[:], rotary), (masks[:], band), (keep[:], keep_in),
            ):
                sp.dma_start(dst, src).then_inc(consts_in, 16)
            def attention_weights(l, wqkv):
                for dst, src in (
                    (wqkv[:, :, 0, :], Wqkv[l, :, 0:INNER].rearrange("p (j n) -> p j n", j=QUADS)),
                    (wqkv[:, :, 1, :], Wqkv[l, :, INNER:2 * INNER].rearrange("p (j n) -> p j n", j=QUADS)),
                    (wqkv[:, :, 2, :], Wqkv[l, :, 2 * INNER:3 * INNER].rearrange("p (j n) -> p j n", j=QUADS)),
                    (wo[:], Wo[l].rearrange("(c p) n -> p c n", p=P)),
                    (scales[:, 0, :], q_scale[l].rearrange("(a n) -> a n", a=1).broadcast_to([P, DH])),
                    (scales[:, 1, :], k_scale[l].rearrange("(a n) -> a n", a=1).broadcast_to([P, DH])),
                ):
                    sp.dma_start(dst, src).then_inc(attn_in, 16)

            attention_weights(0, wqkv_first)
            with sp.Fori(0, DEPTH) as l:
                sp.wait_ge(x_ready, (l + 1) * 2 * B + 1)
                for dst, src in (
                    (w1[:], W1[l]),
                    (w2[:, 0:CH - 1, :], W2[l, 0:(CH - 1) * P, :].rearrange("(c p) n -> p c n", p=P)),
                    (w2[0:HCH[-1][1], CH - 1, :], W2[l, (CH - 1) * P:HID, :]),
                    (fcols[:, 0:1], col(ln_g[l])), (fcols[:, 1:2], col(ln_b[l])), (fcols[:, 2:3], col(b2[l])),
                ):
                    sp.dma_start(dst, src).then_inc(ffn_in, 16)
                for side in range(2):
                    for c, (c0, cn) in enumerate(HCH):
                        k = 3 + side * CH + c
                        sp.dma_start(fcols[0:cn, k:k + 1],
                                     col(b1[l, side * HID + c0:side * HID + c0 + cn])).then_inc(ffn_in, 16)
                sp.wait_ge(y_written, (l + 1) * TILES + 1)
                attention_weights((l + 1) % DEPTH, wqkv)
            with sp.Fori(0, B // 2) as pair:
                for q, result in enumerate((xn, xn_b)):
                    sp.wait_ge(z_out, (pair * 2 + q) * 2 + 2)
                    sp.dma_start(out[pair * 2 + q].rearrange("(n p) d -> p n d", p=P), result[:]).then_inc(out_stored, 16)
            sp.wait_ge(out_stored, B * 16 + 1)

        @blk.vector
        def _(dve):
            def ln_stats(tile, k, call):
                halves = [range(4 * h, 4 * h + 4) for h in range(2)]
                for half in halves:
                    for i in half:
                        last = dve.bn_stats(ln_parts[:, k, i, :], tile(i))
                    last.then_inc(ln_parts_done[k], 1)
                for h, half in enumerate(halves):
                    dve.wait_ge(ln_parts_done[k], call * 2 + h + 1)
                    alone(dve)
                    for i in half:
                        last = dve.bn_aggr(ln_mv[:, k, i, :], ln_parts[:, k, i, :])
                    last.then_inc(ln_mv_done[k], 1)
                for h, half in enumerate(halves):
                    dve.wait_ge(ln_mv_done[k], call * 2 + h + 1)
                    dve.tensor_scalar(ln_var[:, k, 4 * h:4 * h + 4], ln_mv[:, k, 4 * h:4 * h + 4, 1], EPS, None,
                                      ALU.add).then_inc(ln_var_done[k], 1)

            def ln_scale(dst, tile, k, call, done):
                for h in range(2):
                    dve.wait_ge(ln_rs_done[k], call * 2 + h + 1)
                    alone(dve)
                    for i in range(4 * h, 4 * h + 4):
                        last = dve.tensor_scalar(dst(i), tile(i), ln_mv[:, k, i, 0:1], ln_rs[:, k, i:i + 1],
                                                 ALU.subtract, ALU.mult)
                    last.then_inc(done, 1)

            def x_tile(b):
                return lambda i: resid[:, bass.ds(b * TPB + i, 1), :].rearrange("p a d -> p (a d)")

            def tile_of(buffer):
                return lambda i: buffer[:, i, :]

            def quarter(b, h):
                return resid[:, bass.ds(b * TPB + 4 * h, 4), :]

            start_at_one(dve, (rot_done, qsum_done, ssq_done, floor_done, max_done, nbias_done, rsum_done,
                               y_written, z_ln, xw_ready, xw_high, mask_ready))
            dve.memset(half_neg[:], -0.5).then_inc(consts_set, 1)
            dve.memset(X[:], 0.0).then_inc(consts_set, 1)
            dve.memset(Y[:], 0.0).then_inc(consts_set, 1)
            dve.memset(qk[:], 0.0).then_inc(consts_set, 1)
            dve.wait_ge(consts_in, NCONST * 16)
            dve.wait_ge(x_in, B * 16)

            def split_quad(l, j, wqkv):
                quad = bass.ds(j, 1)
                dve.tensor_copy(wqkv_hi[:, quad], wqkv[:, quad]).then_inc(w_high, 1)
                dve.wait_ge(w_high, l * QUADS + j + 1)
                alone(dve)
                dve.tensor_tensor(wqkv_lo[:, quad], wqkv[:, quad], wqkv_hi[:, quad], ALU.subtract).then_inc(w_split, 1)

            ln_stats(x_tile(0), 0, 0)
            with dve.Fori(0, B) as b:
                dve.wait_ge(a_xn2T_ps, b * 2 + 1)
                ln_scale(tile_of(xn), x_tile(b), 0, b, a_xn)
                for i in range(4):
                    dve.wait_ge(a_kv_ps, b * 4 + i + 1)
                    dve.tensor_tensor(kv[:, 2 * i:2 * i + 2, :],
                                      bank[2 + i][:].rearrange("p (t n) -> p t n", t=2),
                                      bkv_sb[:, None, :].broadcast_to([P, 2, 2 * D]), ALU.add).then_inc(a_kv, 1)
                dve.wait_ge(a_state_ps, b + 1)
                dve.tensor_tensor(state[:], bank[6][:, 0:P], block[:, 0, :], ALU.mult).then_inc(a_state, 1)
                ln_stats(x_tile((b + 1) % B), 0, b + 1)
                dve.wait_ge(attn_in, NATTN * 16)
                alone(dve)
                split_quad(0, b, wqkv_first)
                dve.wait_ge(a_ctx, b * 2 + 2)
                dve.tensor_tensor(csum[:, 2:3], csum[:, 0:1], csum[:, 1:2], ALU.add).then_inc(a_csum, 1)
                dve.wait_ge(a_mean_ps, b + 1)
                dve.tensor_scalar(gstat[:, 0:1], bank[7][:, 0:1], -1.0, None, ALU.mult).then_inc(a_mean, 1)
                dve.wait_ge(a_sq, b * 2 + 2)
                dve.tensor_tensor(cssq[:, 2:3], cssq[:, 0:1], cssq[:, 1:2], ALU.add).then_inc(a_ssq, 1)
                dve.wait_ge(a_var_ps, b + 1)
                dve.tensor_scalar(gstat[:, 1:2], bank[7][:, 0:1], EPS, None, ALU.add).then_inc(a_var, 1)
                dve.wait_ge(a_rs, b + 1)
                dve.tensor_tensor(gstat[:, 3:4], gstat[:, 2:3], cols[:, 1:2], ALU.mult).then_inc(a_scale, 1)
                dve.wait_ge(a_scale, b + 1)
                dve.scalar_tensor_tensor(out=gstat[:, 4:5], in0=gstat[:, 3:4], scalar=gstat[:, 0:1],
                                         in1=cols[:, 2:3], op0=ALU.mult, op1=ALU.add).then_inc(a_shift, 1)
                for h in range(2):
                    dve.wait_ge(a_out_ps, b * 2 + h + 1)
                    dve.tensor_tensor(xn[:, 4 * h:4 * h + 4, :], by_tile(bank[4 + h][:]),
                                      bo_sb[:, None, :].broadcast_to([P, 4, D]), ALU.add).then_inc(a_out, 1)
                dve.wait_ge(a_out, b * 2 + 2)
                alone(dve)
                ln_stats(tile_of(xn), 1, b * 2)
                ln_scale(tile_of(scaled), tile_of(xn), 1, b * 2, a_ln2)
                for h in range(2):
                    dve.wait_ge(a_ln2, b * 2 + h + 1)
                    alone(dve)
                    dve.tensor_tensor(quarter(b, h), quarter(b, h), scaled[:, 4 * h:4 * h + 4, :],
                                      ALU.add).then_inc(a_x1, 1)
                dve.wait_ge(a_x1, b * 2 + 2)
                alone(dve)
                ln_stats(x_tile(b), 1, b * 2 + 1)
                ln_scale(tile_of(xn), x_tile(b), 1, b * 2 + 1, a_xn2)

            def make_tables():
                for side in range(2):
                    dve.tensor_tensor(tables[:, :, side, :, :], rotary_sb[:, :, side, :, :],
                                      scales[:, side, None, None, :].broadcast_to([P, TPB, 2, DH]),
                                      ALU.mult).then_inc(tables_set, 1)

            def window_high(l, tile, side):
                dve.tensor_copy(xw[:, side, 0], X[:, bass.ds(column(tile), KW)]).then_inc(xw_high, 1)

            def window_low(l, tile, side):
                dve.wait_ge(xw_high, l * (TILES + 1) + tile + 2)
                alone(dve)
                dve.tensor_tensor(xw[:, side, 1], X[:, bass.ds(column(tile), KW)], xw[:, side, 0],
                                  ALU.subtract).then_inc(xw_ready, 1)

            make_tables()
            dve.wait_ge(x_ready, 2 * B + 1)
            alone(dve)
            window_high(0, 0, 0)
            window_low(0, 0, 0)

            with dve.Fori(0, DEPTH) as l:
                dve.wait_ge(tables_set, l * 2 + 2)
                dve.wait_ge(x_ready, (l + 1) * 2 * B + 1)

                def slot(j, t, n, side):
                    u = l * UNITS + t * QUADS + j + 1
                    r = j % 2
                    if on(n, 6) and j == 1:
                        c = column(t - 2) + WIN
                        dve.wait_ge(y_done, l * TILES + t)
                        dve.tensor_tensor(Y[0:64, bass.ds(c, P)], bank[7][0:64, 0:P],
                                          X[0:64, bass.ds(c, P)], ALU.add)
                        dve.tensor_tensor(Y[64:128, bass.ds(c + 1, P)], bank[7][64:128, 0:P],
                                          X[64:128, bass.ds(c + 1, P)], ALU.add).then_inc(y_written, 1)
                    if on(n, 0) and j == WINDOW_SLOT:
                        dve.wait_ge(v_done, u - j)
                        window_high(l, t + 1, 1 - side)
                    if on(n, 1):
                        q_cos, q_sin = (rot[:, 1 - r, part, 0:QH, :] for part in range(2))
                        dve.wait_ge(rot_done, u)
                        dve.tensor_tensor(q_cos, q_cos, q_sin, ALU.add).then_inc(qsum_done, 1)
                    if on(n, 0) and j == WINDOW_SLOT:
                        window_low(l, t + 1, 1 - side)
                    if on(n, 2) and j == 2:
                        dve.tensor_copy(mask[:], masks[:, bass.ds(t % TPB, 1), :].rearrange(
                            "p a k -> p (a k)")).then_inc(mask_ready, 1)
                    if on(n, 0):
                        dve.wait_ge(square_done, u + 1)
                        dve.tensor_reduce(sumsq[:, r, 0, :], square[:], AX.X, ALU.add).then_inc(ssq_done, 1)
                        dve.wait_ge(ssq_done, u + 1)
                        dve.tensor_scalar(sumsq[:, r, 1, :], sumsq[:, r, 0, :], 1e-24, None,
                                          ALU.max).then_inc(floor_done, 1)
                    if on(n, 0):
                        tab = tables[:, bass.ds(t % TPB, 1), :, :, :].rearrange("p a s c d -> p (a s) c d")
                        heads = bank[0][:].rearrange("p (s h d) -> p s h d", s=2, h=QH)
                        parts = rot[:, r].rearrange("p c (s h) d -> p c s h d", s=2)
                        dve.tensor_tensor(parts[:, 0], heads,
                                          tab[:, :, 0, None, :].broadcast_to([P, 2, QH, DH]), ALU.mult)
                        for a in range(2):
                            here, there = slice(a * HALF, (a + 1) * HALF), slice((1 - a) * HALF, (2 - a) * HALF)
                            last = dve.tensor_tensor(parts[:, 1, :, :, there], heads[:, :, :, here],
                                                     tab[:, :, 1, None, here].broadcast_to([P, 2, QH, HALF]),
                                                     ALU.mult)
                        last.then_inc(rot_done, 1)
                    if on(n, 3):
                        dve.wait_ge(exp_done, u - 2)
                        dve.reciprocal(rsum[:], rowsum[:]).then_inc(rsum_done, 1)
                    if on(n, 2):
                        two = (j - 2) % QUADS
                        if two == 0:
                            dve.wait_ge(mask_ready, l * TILES + t + 2)
                        dve.wait_ge(s_done, u - 1)
                        alone(dve)
                        for h in range(QH):
                            last = dve.tensor_tensor_reduce(
                                scores[:, r, h, :], bank[3 + h % 2][:, (h // 2) * GK:(h // 2 + 1) * GK], mask[:],
                                1.0, -3e38, ALU.add, ALU.max, rowmax[:, h:h + 1])
                        last.then_inc(max_done, 1)
                        dve.wait_ge(max_done, u - 1)
                        dve.scalar_tensor_tensor(out=nbias[:, r], in0=rowmax[:], scalar=-1.0,
                                                 in1=rnorm[:, two, 0:QH], op0=ALU.mult,
                                                 op1=ALU.mult).then_inc(nbias_done, 1)

                def split_w1():
                    dve.wait_ge(ffn_in, (l + 1) * NFFN * 16)
                    dve.tensor_copy(w1_hi[:], w1[:]).then_inc(w1_high, 1)
                    dve.wait_ge(w1_high, l + 1)
                    dve.tensor_tensor(w1_lo[:], w1[:], w1_hi[:], ALU.subtract).then_inc(w1_split, 1)

                def stats(b, h):
                    v = l * 2 * B + b * 2 + h
                    dve.wait_ge(ft_done, v + 1)
                    alone(dve)
                    for i in range(FTT):
                        last = dve.bn_stats(fstat[:, h, i, :], bank[h][:, i * P:(i + 1) * P])
                    last.then_inc(fstat_done, 1)
                    dve.wait_ge(fstat_done, v + 1)
                    alone(dve)
                    for i in range(FTT):
                        last = dve.bn_aggr(fmv[:, h, i, :], fstat[:, h, i, :])
                    last.then_inc(faggr_done, 1)
                    dve.wait_ge(faggr_done, v + 1)
                    dve.tensor_scalar(fvar[:, h], fmv[:, h, :, 1], EPS, None, ALU.add).then_inc(eps_done, 1)

                def normalize(b, h):
                    dve.wait_ge(frs_done, l * 2 * B + b * 2 + h + 1)
                    for i in range(FTT):
                        last = dve.tensor_scalar(fnorm[:, h, i, :], bank[h][:, i * P:(i + 1) * P],
                                                 fmv[:, h, i, 0:1], frs[:, h, i:i + 1], ALU.subtract, ALU.mult)
                    last.then_inc(fnorm_done, 1)

                def gated(b, h, k):
                    c0, cn = HCH[k]
                    dve.wait_ge(gelu_done, (l * 2 * B + b * 2 + h) * CH + k + 1)
                    dve.scalar_tensor_tensor(out=hidden[0:cn, h, k, :], in0=bank[4 + (h + k) % 2][0:cn, :],
                                             scalar=fcols[0:cn, 3 + k:4 + k], in1=gate[0:cn, (h + k) % 2, :],
                                             op0=ALU.add, op1=ALU.mult).then_inc(hid_done, 1)

                def residual(b, h):
                    dve.wait_ge(down_done, l * 2 * B + b * 2 + h + 1)
                    c = b * XB + WIN + h * FT
                    for side in range(2):
                        rows = slice(64 * side, 64 * side + 64)
                        last = dve.scalar_tensor_tensor(
                            out=X[rows, bass.ds(c + side, FT)], in0=bank[6 + h][rows, :],
                            scalar=fcols[rows, 2:3], in1=Y[rows, bass.ds(c + side, FT)],
                            op0=ALU.add, op1=ALU.add)
                    last.then_inc(x_ready, 1)

                def batch(b, ahead):
                    gated(b, 0, 1)
                    if ahead:
                        stats(b + 1, 0)
                    gated(b, 0, 2)
                    gated(b, 1, 0)
                    if ahead:
                        normalize(b + 1, 0)
                        stats(b + 1, 1)
                    residual(b, 0)
                    gated(b, 1, 1)
                    if ahead:
                        normalize(b + 1, 1)
                    gated(b, 1, 2)
                    dve.wait_ge(attn_in, (l + 2) * NATTN * 16)
                    alone(dve)
                    split_quad(l + 1, b, wqkv)
                    if not ahead:
                        dve.wait_ge(x_ready, (l + 2) * 2 * B - 1)
                        alone(dve)
                        window_high(l + 1, 0, 0)
                        window_low(l + 1, 0, 0)
                        make_tables()
                    if ahead:
                        gated(b + 1, 0, 0)
                    residual(b, 1)

                def after(k):
                    if k == 1:
                        split_w1()
                    if k == 2:
                        for h in range(2):
                            stats(0, h)
                        for h in range(2):
                            normalize(0, h)

                pipeline(dve, slot, after)
                gated(0, 0, 0)
                with dve.Fori(0, B - 1) as b:
                    batch(b, True)
                batch(B - 1, False)

            with dve.Fori(0, B // 2) as pair:
                for q, result in enumerate((xn, xn_b)):
                    b = pair * 2 + q
                    dve.wait_ge(z_x_ps, b + 2)
                    alone(dve)

                    def banked(i, q=q):
                        return bank[2 * q + i // 4][:, (i % 4) * D:(i % 4 + 1) * D]

                    ln_stats(banked, 1, b + 2 * B)
                    ln_scale(tile_of(scaled), banked, 1, b + 2 * B, z_ln)
                    if q == 0:
                        dve.wait_ge(out_stored, pair * 32 + 1)
                    for h in range(2):
                        dve.wait_ge(z_ln, b * 2 + h + 2)
                        alone(dve)
                        dve.tensor_tensor(result[:, 4 * h:4 * h + 4, :], scaled[:, 4 * h:4 * h + 4, :], quarter(b, h),
                                          ALU.add).then_inc(z_out, 1)

        @blk.gpsimd
        def _(pool):
            def ln_pow(k, call):
                for h in range(2):
                    half = slice(4 * h, 4 * h + 4)
                    pool.wait_ge(ln_var_done[k], call * 2 + h + 1)
                    alone(pool)
                    pool.tensor_tensor(ln_rs[:, k, half], ln_var[:, k, half], half_neg[:, 0:4],
                                       ALU.pow).then_inc(ln_rs_done[k], 1)

            start_at_one(pool, (rnorm_done, ksum_done, kscale_done, probs_done, tail_moved))
            pool.wait_ge(consts_set, NSET)
            ln_pow(0, 0)
            with pool.Fori(0, B) as b:
                ln_pow(0, b + 1)
                pool.wait_ge(a_var, b + 1)
                pool.tensor_tensor(gstat[:, 2:3], gstat[:, 1:2], half_neg[:, 0:1], ALU.pow).then_inc(a_rs, 1)
                ln_pow(1, b * 2)
                ln_pow(1, b * 2 + 1)

            with pool.Fori(0, DEPTH) as l:
                pool.wait_ge(x_ready, (l + 1) * 2 * B + 1)

                def slot(j, t, n, side):
                    u = l * UNITS + t * QUADS + j + 1
                    r = j % 2
                    if on(n, 4):
                        pool.wait_ge(rsum_done, u - 3)
                        pool.tensor_tensor(probs[:], probs[:], rsum[:, :, None].broadcast_to([P, QH, GK]),
                                           ALU.mult).then_inc(probs_done, 1)
                    if on(n, 1):
                        k_cos, k_sin = (rot[:, 1 - r, part, QH:2 * QH, :] for part in range(2))
                        pool.wait_ge(rot_done, u)
                        pool.tensor_tensor(k_cos, k_cos, k_sin, ALU.add).then_inc(ksum_done, 1)
                        pool.wait_ge(floor_done, u)
                        pool.tensor_tensor(rnorm[:, (j - 1) % QUADS, :], sumsq[:, 1 - r, 1, :],
                                           half_neg[:, 0:2 * QH], ALU.pow).then_inc(rnorm_done, 1)
                        pool.wait_ge(rnorm_done, u)
                        pool.wait_ge(ksum_done, u)
                        pool.tensor_tensor(k_cos, k_cos,
                                           rnorm[:, (j - 1) % QUADS, QH:2 * QH, None].broadcast_to([P, QH, DH]),
                                           ALU.mult).then_inc(kscale_done, 1)
                    if on(n, 0):
                        if on(n, QUADS):
                            pool.wait_ge(s_done, u - 3)
                            alone(pool)
                        pool.tensor_tensor(qk[:, j, 2:4, 0:WIN], qk[:, j, 2:4, P:KW],
                                           keep[:, bass.ds(t % TPB, 1), None].broadcast_to([P, 2, WIN]),
                                           ALU.mult).then_inc(tail_moved, 1)

                pipeline(pool, slot)

                def layer_norm(b):
                    v0 = l * 2 * B + b * 2
                    for h in range(2):
                        pool.wait_ge(eps_done, v0 + h + 1)
                        alone(pool)
                        pool.tensor_tensor(frs[:, h], fvar[:, h], half_neg[:, 0:FTT], ALU.pow).then_inc(frs_done, 1)
                    for h in range(2):
                        pool.wait_ge(faff_done, v0 + h + 1)
                        alone(pool)
                        pool.tensor_tensor(fxn_lo[:, h], fxn[:, h], fxn_hi[:, h], ALU.subtract).then_inc(fsplit_done, 1)

                with pool.Fori(0, B) as b:
                    layer_norm(b)

            with pool.Fori(0, B) as b:
                ln_pow(1, b + 2 * B)

        @blk.scalar
        def _(act):
            start_at_one(act, (square_done, v_kept, pT_kept, qk_kept, exp_done, o_kept, x_ready))
            act.wait_ge(consts_in, NCONST * 16)
            act.wait_ge(consts_set, NSET)
            with act.Fori(0, B) as b:
                for h in range(2):
                    act.wait_ge(a_xnT_ps, b * 2 + h + 1)
                    act.activation(xnT[:, 512 * h:512 * h + 512], bank[h][:], ACT.Copy).then_inc(a_xnT, 1)
                act.wait_ge(a_q_ps, b + 1)
                for h in range(2):
                    act.activation(qT[:, 512 * h:512 * h + 512], bank[h][:], ACT.Identity,
                                   bias=cols[:, 0:1]).then_inc(a_q, 1)
                act.wait_ge(a_ctx_ps, b + 1)
                for h in range(2):
                    act.activation(ctxT[:, 512 * h:512 * h + 512], bank[2 + h][:], ACT.Copy,
                                   accum_out=csum[:, h:h + 1]).then_inc(a_ctx, 1)
                act.wait_ge(a_mean, b + 1)
                act.wait_ge(a_ctx, b * 2 + 2)
                for h in range(2):
                    act.activation(xnT[:, 512 * h:512 * h + 512], ctxT[:, 512 * h:512 * h + 512], ACT.Square,
                                   bias=gstat[:, 0:1], accum_out=cssq[:, h:h + 1]).then_inc(a_sq, 1)
                act.wait_ge(a_shift, b + 1)
                for h in range(2):
                    act.activation(qT[:, 512 * h:512 * h + 512], ctxT[:, 512 * h:512 * h + 512], ACT.Identity,
                                   scale=gstat[:, 3:4], bias=gstat[:, 4:5]).then_inc(a_gn, 1)
                for h in range(2):
                    act.wait_ge(a_xn2T_ps, b * 2 + h + 2)
                    for side in range(2):
                        rows = slice(64 * side, 64 * side + 64)
                        last = act.activation(X[rows, bass.ds(b * XB + WIN + h * 512 + side, 512)],
                                              bank[h][rows, :], ACT.Copy)
                    last.then_inc(x_ready, 1)

            with act.Fori(0, DEPTH) as l:
                def slot(j, t, n, side):
                    u = l * UNITS + t * QUADS + j + 1
                    if on(n, 1):
                        act.wait_ge(v_done, u)
                        if on(n, 5):
                            act.wait_ge(o_done, u - 4)
                        act.activation(vs[:, (j - 1) % QUADS].rearrange("p g c -> p (g c)"),
                                       bank[1][0:GK, :], ACT.Copy).then_inc(v_kept, 1)
                    if on(n, 2):
                        act.wait_ge(tail_moved, u - 1)
                        act.wait_ge(qkT_done, u - 1)
                        act.activation(qk[:, (j - 2) % QUADS, :, WIN:KW], bank[2][:].rearrange("p (c k) -> p c k", c=4),
                                       ACT.Copy).then_inc(qk_kept, 1)
                    if on(n, 0):
                        act.wait_ge(ssq_done, u)
                        act.wait_ge(proj_done, u + 1)
                        act.activation(square[:].rearrange("p h d -> p (h d)"), bank[0][:],
                                       ACT.Square).then_inc(square_done, 1)
                    if on(n, 5):
                        act.wait_ge(o_done, u - 4)
                        act.activation(oT[:, (j - 5) % 2, :], bank[6][:, 0:2 * P], ACT.Copy).then_inc(o_kept, 1)
                    if on(n, 4):
                        act.wait_ge(pT_done, u - 3)
                        act.activation(pT[:], bank[5][0:GK, :], ACT.Copy).then_inc(pT_kept, 1)
                    if on(n, 3):
                        three = (j - 3) % QUADS
                        act.wait_ge(nbias_done, u - 2)
                        for h in range(QH):
                            last = act.activation(probs[:, h, :], scores[:, three % 2, h, :], ACT.Exp,
                                                  bias=nbias[:, three % 2, h:h + 1],
                                                  scale=rnorm[:, three, h:h + 1], accum_out=rowsum[:, h:h + 1])
                        last.then_inc(exp_done, 1)

                def affine(b, h):
                    act.wait_ge(fback_done, l * 2 * B + b * 2 + h + 1)
                    for dst in (fxn, fxn_hi):
                        last = act.activation(dst[:, h], bank[h][:], ACT.Identity, scale=fcols[:, 0:1],
                                              bias=fcols[:, 1:2])
                    last.then_inc(faff_done, 1)

                def copy_y(b, h):
                    act.activation(y_part[:, h], Y[:, bass.ds(b * XB + WIN + h * FT, FT)],
                                   ACT.Identity).then_inc(y_copied, 1)

                def gelu(b, h, k):
                    c0, cn = HCH[k]
                    act.wait_ge(up_done, (l * 2 * B + b * 2 + h) * CH + k + 1)
                    act.activation(gate[0:cn, (h + k) % 2, :], bank[2 + (h + k) % 2][0:cn, :], ACT.Gelu,
                                   bias=fcols[0:cn, 3 + CH + k:4 + CH + k]).then_inc(gelu_done, 1)

                def batch(b, ahead):
                    for h in range(2):
                        if ahead:
                            copy_y(b + 1, h)
                    gelu(b, 0, 1)
                    gelu(b, 0, 2)
                    gelu(b, 1, 0)
                    if ahead:
                        affine(b + 1, 0)
                    gelu(b, 1, 1)
                    gelu(b, 1, 2)
                    if ahead:
                        gelu(b + 1, 0, 0)
                        affine(b + 1, 1)

                def after(k):
                    if k == 0:
                        act.wait_ge(y_written, l * TILES + TPB + 1)
                        alone(act)
                        for h in range(2):
                            copy_y(0, h)

                pipeline(act, slot, after)
                act.wait_ge(ffn_in, (l + 1) * NFFN * 16)
                affine(0, 0)
                affine(0, 1)
                gelu(0, 0, 0)
                act.wait_ge(y_written, (l + 1) * TILES + 1)
                alone(act)
                with act.Fori(0, B - 1) as b:
                    batch(b, True)
                batch(B - 1, False)

            act.wait_ge(x_ready, (DEPTH + 1) * 2 * B + 1)
            alone(act)
            with act.Fori(0, B // 2) as pair:
                for q, straight in enumerate((ctxT, xnT)):
                    b = pair * 2 + q
                    if q == 0:
                        act.wait_ge(z_x_ps, b + 1)
                        alone(act)
                    for side in range(2):
                        rows = slice(64 * side, 64 * side + 64)
                        last = act.activation(straight[rows, :], X[rows, bass.ds(b * XB + WIN + side, S)], ACT.Copy)
                    last.then_inc(z_xT, 1)

        @blk.tensor
        def _(pe):
            start_at_one(pe, (proj_done, v_done, qkT_done, s_done, pT_done, o_done, y_done, a_xn2T_ps, z_x_ps))
            pe.wait_ge(consts_in, NCONST * 16)
            pe.wait_ge(consts_set, NSET)

            def transposes(src, ready, b, done):
                for h in range(2):
                    pe.wait_ge(ready, b * 2 + h + 1)
                    alone(pe)
                    for i in range(4):
                        last = pe.transpose(bank[h][:, i * P:i * P + P], src(4 * h + i), ident[:])
                    last.then_inc(done, 1)

            with pe.Fori(0, B) as b:
                pe.wait_ge(x_ready, b * 2 + 1)
                transposes(lambda i: xn[:, i, :], a_xn, b, a_xnT_ps)
                for i in range(TPB):
                    if i % 4 == 0:
                        pe.wait_ge(a_xnT, b * 2 + i // 4 + 1)
                    last = pe.matmul(bank[2 + i // 2][:, (i % 2) * 2 * D:(i % 2 + 1) * 2 * D],
                                     xnT[:, i * P:i * P + P], wkv_sb[:], start=True, stop=True)
                    if i % 2:
                        last.then_inc(a_kv_ps, 1)
                for h in range(2):
                    last = pe.matmul(bank[h][:], wq_sb[:], xnT[:, 512 * h:512 * h + 512], start=True, stop=True)
                last.then_inc(a_q_ps, 1)
                for i in range(TPB):
                    if i % 2 == 0:
                        pe.wait_ge(a_kv, b * 4 + i // 2 + 1)
                    last = pe.matmul(bank[6][:, 0:P], kv[:, i, 0:D], kv[:, i, D:2 * D],
                                     start=(i == 0), stop=(i == TPB - 1))
                last.then_inc(a_state_ps, 1)
                pe.wait_ge(a_q, b * 2 + 2)
                pe.wait_ge(a_state, b + 1)
                for h in range(2):
                    last = pe.matmul(bank[2 + h][:], state[:], qT[:, 512 * h:512 * h + 512], start=True, stop=True)
                last.then_inc(a_ctx_ps, 1)
                pe.wait_ge(a_csum, b + 1)
                pe.matmul(bank[7][:, 0:1], block[:, 1, :], csum[:, 2:3], start=True, stop=True).then_inc(a_mean_ps, 1)
                pe.wait_ge(a_mean, b + 1)
                pe.wait_ge(a_ssq, b + 1)
                pe.matmul(bank[7][:, 0:1], block[:, 1, :], cssq[:, 2:3], start=True, stop=True).then_inc(a_var_ps, 1)
                pe.wait_ge(a_gn, b * 2 + 2)
                for h in range(2):
                    for i in range(4):
                        t = 4 * h + i
                        last = pe.matmul(bank[4 + h][:, i * D:i * D + D], qT[:, t * P:t * P + P], wout_sb[:],
                                         start=True, stop=True)
                    last.then_inc(a_out_ps, 1)
                transposes(lambda i: xn[:, i, :], a_xn2, b, a_xn2T_ps)

            with pe.Fori(0, DEPTH) as l:
                pe.wait_ge(attn_in, (l + 1) * NATTN * 16)

                def split_product(dst, side, window, j, columns):
                    for i, (part, w) in enumerate(((0, wqkv_hi), (0, wqkv_lo), (1, wqkv_hi))):
                        last = pe.matmul(dst, xw[:, side, part, window],
                                         w[:, j, columns].rearrange("p a n -> p (a n)"),
                                         start=(i == 0), stop=(i == 2))
                    return last

                def slot(j, t, n, side):
                    u = l * UNITS + t * QUADS + j + 1
                    if on(n, 2):
                        pe.wait_ge(qk_kept, u - 2)
                        pe.wait_ge(kscale_done, u - 1)
                        pe.wait_ge(qsum_done, u - 1)
                        for c in range(4):
                            last = pe.transpose(bank[2][:, c * P:c * P + P],
                                                rot[:, j % 2, 0, 2 * c:2 * c + 2].rearrange("p h d -> p (h d)"),
                                                ident[:])
                        last.then_inc(qkT_done, 1)
                    if on(n, 0):
                        if j == 0:
                            pe.wait_ge(xw_ready, l * (TILES + 1) + t + 2)
                        if n is not None:
                            pe.wait_ge(w_split, l * QUADS + j + 1)
                        pe.wait_ge(square_done, u)
                        pe.wait_ge(rot_done, u)
                        split_product(bank[0][:], side, slice(WIN, KW), j, slice(0, 2)).then_inc(proj_done, 1)
                    if on(n, 4):
                        pe.wait_ge(probs_done, u - 3)
                        for h in range(QH):
                            last = pe.transpose(bank[5][0:GK, h * P:h * P + P], probs[:, h, :], ident[:])
                        last.then_inc(pT_done, 1)
                    if on(n, 2):
                        two = (j - 2) % QUADS
                        pe.wait_ge(qk_kept, u - 1)
                        pe.wait_ge(max_done, u - 2)
                        alone(pe)
                        for h in range(QH):
                            rows = slice(64 * (h % 2), 64 * (h % 2) + 64)
                            c = h // 2
                            for g in range(2):
                                last = pe.matmul(bank[3 + h % 2][g * GQ:(g + 1) * GQ, c * GK:(c + 1) * GK],
                                                 qk[rows, two, c, WIN + g * GQ:WIN + (g + 1) * GQ],
                                                 qk[rows, two, 2 + c, g * GQ:g * GQ + GK],
                                                 start=True, stop=True)
                        last.then_inc(s_done, 1)
                    if on(n, 0):
                        pe.wait_ge(v_kept, u)
                        for g in range(2):
                            last = split_product(bank[1][0:GK, g * QC:(g + 1) * QC], side,
                                                 slice(g * GQ, g * GQ + GK), j, slice(2, 3))
                        last.then_inc(v_done, 1)
                    if on(n, 5):
                        five = (j - 5) % QUADS
                        pe.wait_ge(o_kept, u - 4)
                        if five == 0:
                            pe.wait_ge(y_written, l * TILES + t)
                        for c in range(2):
                            last = pe.matmul(bank[7][:, 0:P], wo[:, 2 * five + c, :],
                                             oT[:, (j - 5) % 2, c * P:c * P + P],
                                             start=(five == 0 and c == 0), stop=(five == 3 and c == 1))
                        if five == 3:
                            last.then_inc(y_done, 1)
                    if on(n, 4):
                        pe.wait_ge(pT_kept, u - 3)
                        for h in range(QH):
                            c, side = h // 2, h % 2
                            for g in range(2):
                                last = pe.matmul(bank[6][64 * side:64 * side + 64, c * P + g * GQ:c * P + (g + 1) * GQ],
                                                 vs[:, j, g, h * DH:(h + 1) * DH],
                                                 pT[:, h * P + g * GQ:h * P + (g + 1) * GQ], start=True, stop=True)
                        last.then_inc(o_done, 1)

                def to_tokens(b, h, free):
                    v = l * 2 * B + b * 2 + h
                    pe.wait_ge(y_copied, v + 1)
                    if free:
                        pe.wait_ge(faff_done, v - 1)
                    alone(pe)
                    for i in range(FTT):
                        last = pe.transpose(bank[h][:, i * P:(i + 1) * P], y_part[:, h, i * P:(i + 1) * P], ident[:])
                    last.then_inc(ft_done, 1)

                def to_features(b, h):
                    pe.wait_ge(fnorm_done, l * 2 * B + b * 2 + h + 1)
                    for i in range(FTT):
                        last = pe.transpose(bank[h][:, i * P:(i + 1) * P], fnorm[:, h, i, :], ident[:])
                    last.then_inc(fback_done, 1)

                def up(b, h, k, crossing=False):
                    c0, cn = HCH[k]
                    v = l * 2 * B + b * 2 + h
                    if k == 0:
                        pe.wait_ge(faff_done, v + 1)
                    if h or k == 2 or crossing:
                        pe.wait_ge(hid_done, v * CH + k - 1)
                    alone(pe)
                    sides = ((bank[2 + (h + k) % 2], HID + c0), (bank[4 + (h + k) % 2], c0))
                    for dst, c in sides:
                        for i, w in enumerate((w1_hi, w1_lo)):
                            pe.matmul(dst[0:cn, :], w[:, c:c + cn], fxn_hi[:, h], start=(i == 0), stop=False)
                    if k == 0:
                        pe.wait_ge(fsplit_done, v + 1)
                        alone(pe)
                    for dst, c in sides:
                        last = pe.matmul(dst[0:cn, :], w1_hi[:, c:c + cn], fxn_lo[:, h], start=False, stop=True)
                    last.then_inc(up_done, 1)

                def down(b, h):
                    pe.wait_ge(hid_done, (l * 2 * B + b * 2 + h + 1) * CH)
                    for k, (c0, cn) in enumerate(HCH):
                        last = pe.matmul(bank[6 + h][:], w2[0:cn, k, :], hidden[0:cn, h, k, :],
                                         start=(k == 0), stop=(k == CH - 1))
                    last.then_inc(down_done, 1)

                def batch(b, ahead):
                    up(b, 0, 1)
                    if ahead:
                        to_tokens(b + 1, 0, True)
                    up(b, 0, 2)
                    up(b, 1, 0)
                    if ahead:
                        to_tokens(b + 1, 1, True)
                    down(b, 0)
                    if ahead:
                        to_features(b + 1, 0)
                    up(b, 1, 1)
                    up(b, 1, 2)
                    if ahead:
                        up(b + 1, 0, 0, True)
                        to_features(b + 1, 1)
                    down(b, 1)

                def after(k):
                    if k == 1:
                        pe.wait_ge(square_done, (l + 1) * UNITS + 1)
                        pe.wait_ge(rot_done, (l + 1) * UNITS + 1)
                        pe.wait_ge(v_kept, (l + 1) * UNITS + 1)
                        to_tokens(0, 0, False)
                        to_tokens(0, 1, False)
                    if k == 3:
                        to_features(0, 0)
                        to_features(0, 1)

                pipeline(pe, slot, after)
                pe.wait_ge(ffn_in, (l + 1) * NFFN * 16)
                pe.wait_ge(w1_split, l + 1)
                pe.wait_ge(y_written, (l + 1) * TILES + 1)
                alone(pe)
                up(0, 0, 0)
                with pe.Fori(0, B - 1) as b:
                    batch(b, True)
                batch(B - 1, False)

            with pe.Fori(0, B // 2) as pair:
                for q, straight in enumerate((ctxT, xnT)):
                    pe.wait_ge(z_xT, pair * 2 + q + 1)
                    if q == 0:
                        pe.wait_ge(z_ln, pair * 4 + 1)
                    alone(pe)
                    for i in range(TPB):
                        last = pe.transpose(bank[2 * q + i // 4][:, (i % 4) * P:(i % 4 + 1) * P],
                                            straight[:, i * P:i * P + P], ident[:])
                    last.then_inc(z_x_ps, 1)


def rotary_tables():
    half = np.arange(0, DH, 2, dtype=np.float32)
    inv_freq = (1.0 / np.float32(10000.0) ** (half / np.float32(DH))).astype(np.float32)
    t = np.arange(S, dtype=np.float32)
    freqs = (t[:, None] * inv_freq[None, :]).astype(np.float64)
    base = ((half + np.float32(0.4 * DH)) / np.float32(1.4 * DH)).astype(np.float64)
    power = ((t - S // 2) / (WIN // 2)).astype(np.float64)
    scale = base[None, :] ** power[:, None]
    tab = np.zeros((S, 2, 2, DH), np.float64)
    for side, s in enumerate((scale * 8.0, 1.0 / scale)):
        tab[:, side, 0, :HALF] = tab[:, side, 0, HALF:] = np.cos(freqs) * s
        tab[:, side, 1, :HALF] = np.sin(freqs) * s
        tab[:, side, 1, HALF:] = -np.sin(freqs) * s
    return np.ascontiguousarray(tab.reshape(TPB, P, 2, 2, DH).transpose(1, 0, 2, 3, 4)).astype(np.float32)


def band_masks():
    q = (np.arange(P) % GQ)[:, None, None]
    k = np.arange(GK)[None, None, :] - WIN
    first = (np.arange(TPB) == 0)[None, :, None] & (np.arange(P) < GQ)[:, None, None]
    seen = (k <= q) & (k >= q - WIN) & ~(first & (k < 0))
    return np.where(seen, np.float32(0), np.float32(MASKED)).astype(np.float32)


def kernel(**inputs):
    import concourse.bacc as bacc
    from concourse.bass_utils import run_bass_kernel_spmd

    a = {k: np.ascontiguousarray(v) for k, v in inputs.items()}
    w = a["L0_attn_Wqkv_w"]
    group = np.arange(P) // A_HEAD
    same = (group[:, None] == group[None, :]).astype(np.float32)
    arrays = {
        "x": a["L0_attn_x"],
        "wkv_t": np.ascontiguousarray(w[D:].T), "bkv": a["L0_attn_Wqkv_b"][D:],
        "wq_t": np.ascontiguousarray(w[:D].T), "bq": a["L0_attn_Wqkv_b"][:D],
        "gn_w": a["L0_attn_gn_w"], "gn_b": a["L0_attn_gn_b"],
        "wo_t": np.ascontiguousarray(a["L0_attn_out_w"].T), "bo": a["L0_attn_out_b"],
    }
    arrays |= {k: a["L0_ffn_" + k] for k in
               ("Wqkv", "q_scale", "k_scale", "Wo", "ln_g", "ln_b", "W1", "b1", "W2", "b2")}
    arrays |= {
        "rotary": rotary_tables(), "band": band_masks(), "ident_in": np.eye(P, dtype=np.float32),
        "keep_in": np.ascontiguousarray(np.broadcast_to(np.arange(TPB) > 0, (P, TPB)).astype(np.float32)),
        "block_in": np.ascontiguousarray(np.stack([same, same / np.float32(A_HEAD * S)], axis=1)),
    }
    nc = bacc.Bacc("TRN2", target_bir_lowering=False, num_devices=1)
    arrays = {f"in_{k}": np.ascontiguousarray(v) for k, v in arrays.items()}
    args = {k[3:]: nc.dram_tensor(k, v.shape, F32, kind="ExternalInput").ap() for k, v in arrays.items()}
    out = nc.dram_tensor("out_x", (B, S, D), F32, kind="ExternalOutput").ap()
    kernel_program(nc, out=out, **args)
    r = run_bass_kernel_spmd(nc, [arrays], core_ids=[0])
    return r.results[0]["out_x"]
```
